# Optimizing a Trainium2 kernel written in Bass

```python
import numpy as np
import jax
import jax.numpy as jnp

def _softmax(x, axis=-1):
    return jax.nn.softmax(x, axis=axis)

def _gelu(x):
    return jax.nn.gelu(x, approximate=True)

def _silu(x):
    return jax.nn.silu(x)

def _sigmoid(x):
    return jax.nn.sigmoid(x)

def _layernorm(x, axis=-1, eps=1e-05):
    m = jnp.mean(x, axis=axis, keepdims=True)
    v = jnp.var(x, axis=axis, keepdims=True)
    return (x - m) / jnp.sqrt(v + eps)

def _scatter_add(tgt, idx, src, axis=0):
    return tgt.at[idx].add(src)

def _segment_sum(src, seg, n):
    return jax.ops.segment_sum(src, seg, n)
kernel_name = 'mk_xattn_ffn_d1_seqx_r8_02cea0'

def setup_inputs(seed: int=0):
    np.random.seed(seed)
    _w = jnp.asarray

    def _rec_inputs():
        import jax
        import jax.numpy as jnp
        _rk = jax.random.key(seed)
        x = -0.0003929 + 0.9999 * jax.random.normal(jax.random.fold_in(_rk, 1), (32, 56, 128), jnp.float32)
        _lenS = 56 - jax.random.randint(jax.random.fold_in(_rk, 7), (32,), 0, max(1, 56 // 4) + 1, jnp.int32)
        _lenS2 = 1500 - jax.random.randint(jax.random.fold_in(_rk, 8), (32,), 0, max(1, 1500 // 4) + 1, jnp.int32)
        _ctx_1024P = jax.random.normal(jax.random.fold_in(_rk, 11), (32, 16, 128), jnp.float32)
        _ctx_1024c = jax.random.dirichlet(jax.random.fold_in(_rk, 511), 0.3 * jnp.ones((16,), jnp.float32), (32, 1500))
        _ctx_1024t = jnp.einsum('bsk,bkd->bsd', _ctx_1024c, _ctx_1024P)
        _ctx_1024t = _ctx_1024t * jax.lax.rsqrt(jnp.mean(jnp.square(_ctx_1024t)) + 1e-12) * 0.953939
        ctx_1024 = 2.81802e-05 + 1.00001 * (_ctx_1024t + 0.3 * jax.random.normal(jax.random.fold_in(_rk, 611), (32, 1500, 128), jnp.float32))
        return (x, ctx_1024)
    x, ctx_1024 = _rec_inputs()

    def _L0_xattn_setup():
        import jax, jax.numpy as jnp
        import numpy as np
        B, S, C = (8, 256, 128)
        key = jax.random.key(seed)
        ks = jax.random.split(key, 9)
        scale = 1.0 / np.sqrt(C)
        return {'x1': jax.random.normal(ks[0], (B, S, C), jnp.float32), 'x2': jax.random.normal(ks[1], (B, S, C), jnp.float32), 'x3': jax.random.normal(ks[2], (B, S, C), jnp.float32), 'Wq': jax.random.normal(ks[3], (C, C), jnp.float32) * scale, 'bq': jax.random.normal(ks[4], (C,), jnp.float32) * scale, 'Wk': jax.random.normal(ks[5], (C, C), jnp.float32) * scale, 'bk': jax.random.normal(ks[6], (C,), jnp.float32) * scale, 'Wv': jax.random.normal(ks[7], (C, C), jnp.float32) * scale, 'bv': jax.random.normal(ks[8], (C,), jnp.float32) * scale}
    _L0_xattn_all = _L0_xattn_setup()
    _L0_xattn_in = {k: v for k, v in _L0_xattn_all.items() if k in ('Wq', 'bq', 'Wk', 'bk', 'Wv', 'bv')}
    del _L0_xattn_all

    def _L0_ffn_setup():
        import jax, jax.numpy as jnp
        import numpy as np
        B, T, DIM = (2, 256, 128)
        H, DH, E, K = (16, 64, 8, 2)
        key = jax.random.key(seed)
        ks = jax.random.split(key, 7)
        s = 0.02
        return {'x': jax.random.normal(ks[0], (B, T, DIM), jnp.float32), 'Wq': jax.random.normal(ks[1], (H, DH, DIM), jnp.float32) * s, 'Wk': jax.random.normal(ks[2], (H, DH, DIM), jnp.float32) * s, 'Wv': jax.random.normal(ks[3], (E, DH, DIM), jnp.float32) * s, 'Ws': jax.random.normal(ks[4], (H, E, DIM), jnp.float32) * s, 'Wd': jax.random.normal(ks[5], (H, E, DIM), jnp.float32) * s, 'Wo': jax.random.normal(ks[6], (E, DIM, DH), jnp.float32) * s}
    _L0_ffn_all = _L0_ffn_setup()
    _L0_ffn_in = {k: v for k, v in _L0_ffn_all.items() if k in ('Wq', 'Wk', 'Wv', 'Ws', 'Wd', 'Wo')}
    del _L0_ffn_all
    return {'x': x, 'ctx_1024': ctx_1024, 'L0_xattn_Wq': _L0_xattn_in['Wq'], 'L0_xattn_bq': _L0_xattn_in['bq'], 'L0_xattn_Wk': _L0_xattn_in['Wk'], 'L0_xattn_bk': _L0_xattn_in['bk'], 'L0_xattn_Wv': _L0_xattn_in['Wv'], 'L0_xattn_bv': _L0_xattn_in['bv'], 'L0_ffn_Wq': _L0_ffn_in['Wq'], 'L0_ffn_Wk': _L0_ffn_in['Wk'], 'L0_ffn_Wv': _L0_ffn_in['Wv'], 'L0_ffn_Ws': _L0_ffn_in['Ws'], 'L0_ffn_Wd': _L0_ffn_in['Wd'], 'L0_ffn_Wo': _L0_ffn_in['Wo']}

def reference(x, ctx_1024, L0_xattn_Wq, L0_xattn_bq, L0_xattn_Wk, L0_xattn_bk, L0_xattn_Wv, L0_xattn_bv, L0_ffn_Wq, L0_ffn_Wk, L0_ffn_Wv, L0_ffn_Ws, L0_ffn_Wd, L0_ffn_Wo):
    import jax
    import jax.numpy as jnp

    def _L0_xattn_ref(x1, x2, x3, Wq, bq, Wk, bk, Wv, bv):
        import jax, jax.numpy as jnp
        import numpy as np
        B, S, C = (8, 256, 128)
        q = jnp.einsum('bsc,dc->bsd', x1, Wq) + bq
        k = jnp.einsum('bsc,dc->bsd', x2, Wk) + bk
        v = jnp.einsum('bsc,dc->bsd', x3, Wv) + bv
        scores = jnp.einsum('bqd,bkd->bqk', q, k)
        attn = jax.nn.softmax(scores, axis=-1)
        return jnp.einsum('bqk,bkd->bqd', attn, v)

    def _L0_ffn_ref(x, Wq, Wk, Wv, Ws, Wd, Wo):
        import jax, jax.numpy as jnp
        import numpy as np
        B, T, DIM = (2, 256, 128)
        H, DH, E, K = (16, 64, 8, 2)
        scale = DH ** (-0.5)
        q = jnp.einsum('btc,hdc->bhtd', x, Wq)
        k = jnp.einsum('btc,hdc->bhtd', x, Wk)
        gate_v = jnp.einsum('btc,hec->bthe', x, Ws)
        w, sel = jax.lax.top_k(gate_v, K)
        wsig = jax.nn.sigmoid(w)
        oh = jax.nn.one_hot(sel, E, dtype=x.dtype)
        mix_v = jnp.einsum('bthk,bthke->bthe', wsig, oh)
        proj_v = jnp.einsum('btc,edc->bted', x, Wv)
        v = jnp.einsum('bthe,bted->bhtd', mix_v, proj_v)
        scores = jnp.einsum('bhid,bhjd->bhij', q * scale, k)
        probs = jax.nn.softmax(scores, axis=-1)
        attn = jnp.einsum('bhij,bhjd->bihd', probs, v)
        gate_o = jnp.einsum('btc,hec->bthe', x, Wd)
        _, sel_o = jax.lax.top_k(gate_o, K)
        mask_o = jax.nn.one_hot(sel_o, E, dtype=x.dtype).sum(axis=3)
        res = jnp.einsum('bthe,bthd,efd->bthf', mask_o, attn, Wo)
        return res.sum(axis=2)
    x = x + _L0_xattn_ref(_layernorm(x, axis=-1), ctx_1024, ctx_1024, L0_xattn_Wq, L0_xattn_bq, L0_xattn_Wk, L0_xattn_bk, L0_xattn_Wv, L0_xattn_bv)
    x = x + _L0_ffn_ref(_layernorm(x, axis=-1), L0_ffn_Wq, L0_ffn_Wk, L0_ffn_Wv, L0_ffn_Ws, L0_ffn_Wd, L0_ffn_Wo)
    return x

_drawn_inputs = setup_inputs


def setup_inputs(seed=0):
    import zlib

    import numpy as np

    out = dict(_drawn_inputs(seed))
    spreads = {}
    factors = {'L0_xattn_bk': 8.0, 'L0_ffn_Wq': 8.0, 'L0_ffn_Wk': 8.0, 'L0_ffn_Ws': 3.12}
    for name, (base, spread) in spreads.items():
        noise = np.random.default_rng([zlib.crc32(name.encode()), seed]).standard_normal(out[name].shape)
        drawn = base * np.exp(spread * noise) if base else spread * noise
        out[name] = jnp.asarray(drawn.astype(out[name].dtype))
    for name, factor in factors.items():
        out[name] = (out[name] * factor).astype(out[name].dtype)
    return out
```

```python
from contextlib import ExitStack

import concourse.bass as bass
from concourse import mybir

F32 = mybir.dt.float32
F16 = mybir.dt.float16
BF16 = mybir.dt.bfloat16
ALU = mybir.AluOpType
ACT = mybir.ActivationFunctionType
AX = mybir.AxisListType

P = 128
BANK = 512


def xattn_ffn(
    nc: bass.Bass,
    x: bass.AP,
    ctx: bass.AP,
    wq: bass.AP,
    bq: bass.AP,
    wk: bass.AP,
    bk: bass.AP,
    wv: bass.AP,
    bv: bass.AP,
    fwq: bass.AP,
    fwk: bass.AP,
    fwv: bass.AP,
    fws: bass.AP,
    fwd: bass.AP,
    fwo: bass.AP,
    out: bass.AP,
):
    B, S, C = x.shape
    L = ctx.shape[1]
    H, DH, _ = fwq.shape
    E = fwv.shape[0]
    assert C == P and S == 56 and H == 16 and DH == 64 and E == 8
    NP = B // 2
    SLOT = 64
    HALF = S // 2
    TK = -(-L // P)
    RPP = L // P
    REST = L - RPP * P
    DUP = P - REST
    EPS = 1e-5
    SCALE = float(DH) ** -0.5
    HG = H // 4
    NQ = 4
    K16 = 2 * HG

    x_v = x.rearrange("(p b) t c -> b t p c", b=2)
    out_v = out.rearrange("(p b) t c -> b t p c", b=2)

    es = ExitStack()
    with es:
        def sb(name, shape, dt=F32):
            return es.enter_context(nc.sbuf_tensor(name, shape, dt))

        def sem(name):
            return es.enter_context(nc.semaphore(name))

        ps = es.enter_context(nc.psum_tensor("ps", [P, 8, BANK], F32))

        ident = sb("ident", [P, P])
        ident16 = sb("ident16", [P, P], F16)
        diag_q = sb("diag_q", [P, S])
        ones16 = sb("ones16", [P, 1], F16)
        rows_of = sb("rows_of", [P, 2, P], BF16)
        diag_h = sb("diag_h", [P, HALF, H])
        diag_e = sb("diag_e", [P, HALF, E], F16)
        rank = sb("rank", [P, 32, E], F16)

        x_all = sb("x_all", [P, NP * C])
        x2_all = sb("x2_all", [P, NP * C])
        y_all = sb("y_all", [P, NP * C])
        bv_all = sb("bv_all", [P, C])
        bq_col = sb("bq_col", [P, 1])
        bk_col = sb("bk_col", [P, 1])
        st_sum = sb("st_sum", [P, NP])
        st_mean = sb("st_mean", [P, NP])
        st_var = sb("st_var", [P, NP])
        st_ve = sb("st_ve", [P, NP])
        st_std = sb("st_std", [P, NP])
        st_rstd = sb("st_rstd", [P, NP])

        wq_nat = sb("wq_nat", [P, C])
        wk_nat = sb("wk_nat", [P, C])
        wv_nat = sb("wv_nat", [P, C])
        wqT = sb("wqT", [P, C])
        wvT = sb("wvT", [P, C])
        xn1T = sb("xn1T", [P, B * S])
        qT = sb("qT", [P, B, SLOT])
        qk_all = sb("qk_all", [P, 2, B * S], F16)
        cq = sb("cq", [P, NP])

        ctxf_all = sb("ctxf_all", [P, 4 * TK * C])
        ctxf = [ctxf_all[:, TK * C * k:TK * C * (k + 1)] for k in range(4)]
        nat = [sb(f"nat{k}", [P, 2, TK * C], F16) for k in range(4)]
        ctxT = [sb(f"ctxT{b}", [P, 2 * TK * P], F16) for b in range(2)]
        qk_cur = [sb(f"qk_cur{s}", [P, 2, 2 * S], F16) for s in range(2)]
        tmax = sb("tmax", [P, 2, SLOT])
        m_q = sb("m_q", [P, 1])
        nshift = sb("nshift", [P, 1])
        dg = sb("dg", [P, 2, S], BF16)
        pf = [sb(f"pf{b}", [P, TK, S]) for b in range(2)]
        p16 = sb("p16", [P, 2, TK, 2, SLOT], F16)
        rden = sb("rden", [P, 1])
        aoT = sb("aoT", [P, 2, SLOT])
        bst = sb("bst", [P, 6])
        mv_all = sb("mv_all", [P, NP * 2])
        mv_cur = sb("mv_cur", [P, 2])
        x2_cur = sb("x2_cur", [P, C])

        fwq_nat = sb("fwq_nat", [P, H // 2, C])
        fwk_nat = sb("fwk_nat", [P, H // 2, C])
        fwv_nat = sb("fwv_nat", [P, E // 2, C])
        fws_nat = sb("fws_nat", [P, C])
        fwd_nat = sb("fwd_nat", [P, C])
        fwo_nat = sb("fwo_nat", [P, E, 2, DH])
        mT = sb("mT", [P, H, C])
        wg = sb("wg", [P, 4, 2, HG, E])
        fwvT = sb("fwvT", [P, E, DH])
        wo2 = sb("wo2", [P, E, C])

        xn = sb("xn", [P, C])
        xnT = sb("xnT", [P, 2 * S + 4])
        z = xn1T[:, :].rearrange("p (h n) -> p h n", h=H)
        g_sb = sb("g_sb", [P, 32, E])
        th = sb("th", [P, NQ * HG, E])
        sg = sb("sg", [P, NQ * HG, E])
        m1 = sb("m1", [P, 32])
        eq1 = sb("eq1", [P, 32, E], F16)
        r1 = sb("r1", [P, 32, E], F16)
        s1 = sb("s1", [P, 32], F16)
        oh1 = sb("oh1", [P, 32, E], F16)
        g2 = sb("g2", [P, 32, E])
        m2 = sb("m2", [P, 32])
        eq2 = sb("eq2", [P, 32, E], F16)
        r2 = sb("r2", [P, 32, E], F16)
        s2 = sb("s2", [P, 32], F16)
        oh2 = sb("oh2", [P, 32, E], F16)
        chosen = sb("chosen", [P, 2 * NQ * HG, E], F16)
        mix = sb("mix", [P, NQ, HG, E])
        mixp = sb("mixp", [P, NQ * 2, H])
        n_dv, n_dm, n_pj = NQ * 2 * HALF * H, NQ * HG * HALF * E // 2, NQ * 2 * DH
        assert n_dv + n_dm + n_pj <= 4 * TK * C
        dv = ctxf_all[:, 0:n_dv].rearrange("p (k t h) -> p k t h", k=NQ * 2, h=H)
        dm = ctxf_all[:, n_dv:n_dv + n_dm].bitcast(F16).rearrange("p (k t e) -> p k t e", k=NQ * HG, e=E)
        pj = ctxf_all[:, n_dv + n_dm:n_dv + n_dm + n_pj].rearrange("p (k d) -> p k d", d=DH)
        smx = sb("smx", [P, 2 * K16])
        ssub = sb("ssub", [P, 2 * K16, S])
        e_sb = sb("e_sb", [P, K16, 2, SLOT])
        rs = sb("rs", [P, K16 * 2])
        rinv = sb("rinv", [P, K16 * 2])
        eT = sb("eT", [P, K16, P])
        vT = sb("vT", [P, H // 2, 2, SLOT])
        v_sb = sb("v_sb", [P, H, DH])
        attnf = sb("attnf", [P, 2 * K16, DH])
        ah = sb("ah", [P, 2 * K16, 2, DH], F16)
        aT = sb("aT", [P, E, 2, SLOT])

        d_x = sem("d_x")
        d_w = sem("d_w")
        d_fw = sem("d_fw")
        d_ctx = [sem(f"d_ctx{k}") for k in range(4)]
        d_out = sem("d_out")
        c_zero = sem("c_zero")
        c_id = sem("c_id")
        c_dve = sem("c_dve")
        ln = sem("ln")
        ln_sqrt = sem("ln_sqrt")
        su_pe = sem("su_pe")
        su_act = sem("su_act")
        su_dve = sem("su_dve")
        qkc = sem("qkc")
        nathi = sem("nathi")
        natlo = sem("natlo")
        natlo2 = sem("natlo2")
        tfull = sem("tfull")
        tev_d = sem("tev_d")
        tev_a = sem("tev_a")
        st_done = sem("st_done")
        tmx = sem("tmx")
        tmT = sem("tmT")
        mred = sem("mred")
        nsh = sem("nsh")
        dghi = sem("dghi")
        dgr = sem("dgr")
        shd = sem("shd")
        expd = sem("expd")
        plo = sem("plo")
        pvd = sem("pvd")
        rdn = sem("rdn")
        aor = sem("aor")
        prj = sem("prj")
        x2d = sem("x2d")
        bsd = sem("bsd")
        mvd = sem("mvd")
        mvc = sem("mvc")
        x2c = sem("x2c")
        l2a = sem("l2a")
        l2b = sem("l2b")
        l2c = sem("l2c")
        f_xn = sem("f_xn")
        f_xnT = sem("f_xnT")
        f_xnTe = sem("f_xnTe")
        f_g = sem("f_g")
        f_ge = sem("f_ge")
        f_th = sem("f_th")
        f_pj = sem("f_pj")
        f_pje = sem("f_pje")
        f_z1 = sem("f_z1")
        f_z2 = sem("f_z2")
        f_z1e = sem("f_z1e")
        f_z2e = sem("f_z2e")
        f_s = sem("f_s")
        f_mx = sem("f_mx")
        f_sub = sem("f_sub")
        f_e = sem("f_e")
        f_rs = sem("f_rs")
        f_ri = sem("f_ri")
        f_top = sem("f_top")
        f_mo = sem("f_mo")
        f_sg = sem("f_sg")
        f_mix = sem("f_mix")
        f_tr = sem("f_tr")
        f_tre = sem("f_tre")
        f_d = sem("f_d")
        f_dm = sem("f_dm")
        f_et = sem("f_et")
        f_ete = sem("f_ete")
        f_vt = sem("f_vt")
        f_vte = sem("f_vte")
        f_vv = sem("f_vv")
        f_vve = sem("f_vve")
        f_pv = sem("f_pv")
        f_nrm = sem("f_nrm")
        f_ahi = sem("f_ahi")
        f_alo = sem("f_alo")
        f_a = sem("f_a")
        f_ae = sem("f_ae")
        f_o = sem("f_o")
        f_y = sem("f_y")
        t_ = [sem(f"top_step{n}") for n in range(10)]


        def after(eng, s, value):
            if not isinstance(value, int) or value > 0:
                eng.wait_ge(s, value)

        NW, NFW = 6, 7
        NG = 4
        GW = B * S // NG
        SU_QV, SU_G, SU_V, SU_O, SU_M, SU_X = 1, 2, 3, 4, 5, 6

        block = es.enter_context(nc.Block())

        @block.sync
        def _(sp):
            sp.wait_ge(c_zero, 1)
            for b in range(2):
                sp.dma_start(x_all[SLOT * b:SLOT * b + S, :].rearrange("t (p c) -> t p c", c=C), x_v[b]).then_inc(d_x, 16)
            for dst, src in ((wq_nat[:, :], wq), (wk_nat[:, :], wk), (wv_nat[:, :], wv),
                             (bq_col[:, :], bq.rearrange("(d o) -> d o", o=1)), (bk_col[:, :], bk.rearrange("(d o) -> d o", o=1)),
                             (bv_all[:, :], bv.rearrange("(o d) -> o d", o=1).broadcast_to((P, C)))):
                sp.dma_start(dst, src).then_inc(d_w, 16)

            def load(k, n):
                sp.dma_start(ctxf[k][:, 0:RPP * C], ctx[n, 0:RPP * P, :].rearrange("(p r) c -> p (r c)", r=RPP)).then_inc(d_ctx[k], 16)
                sp.dma_start(ctxf[k][0:REST, RPP * C:], ctx[n, RPP * P:L, :]).then_inc(d_ctx[k], 16)
                sp.dma_start(ctxf[k][REST:P, RPP * C:], ctx[n, L - DUP:L, :]).then_inc(d_ctx[k], 16)

            for dst, src in (
                (fwq_nat[:, :, :], fwq.rearrange("(k h) d c -> (h d) k c", h=2)),
                (fwk_nat[:, :, :], fwk.rearrange("(k h) d c -> (h d) k c", h=2)),
                (fwv_nat[:, :, :], fwv.rearrange("(k e) d c -> (e d) k c", e=2)),
                (fws_nat[:, :], fws.rearrange("h e c -> (h e) c")),
                (fwd_nat[:, :], fwd.rearrange("h e c -> (h e) c")),
                (fwo_nat[:, :, 0, :], fwo.rearrange("e f d -> f e d")),
                (fwo_nat[:, :, 1, :], fwo.rearrange("e f d -> f e d")),
            ):
                sp.dma_start(dst, src).then_inc(d_fw, 16)
            for k in range(4):
                load(k, k)

            def loads(i):
                for k in range(4):
                    n = 4 * i + k
                    after(sp, nathi, n - 3)
                    after(sp, natlo, n - 3)
                    after(sp, natlo2, n - 3)
                    sp_load(k, n)

            def sp_load(k, n):
                flat = ctx.rearrange("n l c -> (n l) c")
                sp.dma_start(ctxf[k][:, 0:RPP * C],
                             flat[bass.ds(n * L, RPP * P), :].rearrange("(p r) c -> p (r c)", r=RPP)).then_inc(d_ctx[k], 16)
                sp.dma_start(ctxf[k][0:REST, RPP * C:], flat[bass.ds(n * L + RPP * P, REST), :]).then_inc(d_ctx[k], 16)
                sp.dma_start(ctxf[k][REST:P, RPP * C:], flat[bass.ds(n * L + L - DUP, DUP), :]).then_inc(d_ctx[k], 16)

            with sp.Fori(1, NP // 2) as i:
                loads(i)
            with sp.Fori(0, NP) as i:
                after(sp, f_y, i + 1)
                for b in range(2):
                    sp.dma_start(out.rearrange("n t c -> (n t) c")[bass.ds(i * (2 * S) + b * S, S), :],
                                 y_all[SLOT * b:SLOT * b + S, bass.ds(i * C, C)]).then_inc(d_out, 16)
            sp.wait_ge(d_out, 32 * NP)

        @block.gpsimd
        def _(pool):
            pool.memset(x_all[:, :], 0.0).then_inc(c_zero, 1)
            pool.memset(ident[:, :], 0.0).then_inc(c_id, 1)
            pool.wait_ge(c_id, 1)
            pool.affine_select(out=ident[:, :], in_=ident[:, :], compare_op=ALU.not_equal, fill=1.0, base=0,
                               pattern=[[-1, P]], channel_multiplier=1).then_inc(c_id, 1)
            pool.memset(qT[:, :, :], 0.0).then_inc(c_zero, 1)
            pool.memset(tmax[:, :, :], 0.0).then_inc(c_zero, 1)
            pool.memset(p16[:, 0, :, :, :], 1.0).then_inc(c_zero, 1)
            pool.memset(p16[:, 1, :, :, :], 0.0).then_inc(c_zero, 1)
            pool.memset(aoT[:, :, :], 0.0).then_inc(c_zero, 1)
            pool.memset(rows_of[:, :, :], 0.0).then_inc(c_zero, 1)
            pool.memset(ones16[:, :], 1.0).then_inc(c_zero, 1)
            pool.wait_ge(c_zero, 8)
            for b in range(2):
                pool.memset(rows_of[SLOT * b:SLOT * b + SLOT, b, :], -1.0).then_inc(c_zero, 1)
            pool.wait_ge(c_zero, 10)
            for e in range(E):
                pool.memset(rank[:, :, e], float(E - e)).then_inc(c_zero, 1)
            pool.memset(e_sb[:, :, :, :], 0.0).then_inc(c_zero, 1)
            pool.memset(vT[:, :, :, :], 0.0).then_inc(c_zero, 1)
            pool.memset(aT[:, :, :, :], 0.0).then_inc(c_zero, 1)
            pool.memset(xnT[:, :], 0.0).then_inc(c_zero, 1)

            def low_rows(n, k):
                after(pool, nathi, n + 1)
                pool.tensor_tensor(nat[k][:, 1, 8 * C:], ctxf[k][:, 8 * C:], nat[k][:, 0, 8 * C:], ALU.subtract).then_inc(natlo2, 1)

            def low_probs(n, b):
                after(pool, expd, 2 * n + 2)
                after(pool, pvd, n - 1)
                pool.tensor_tensor(p16[:, 1, :, b, 0:S], pf[b][:, :, :], p16[:, 0, :, b, 0:S], ALU.subtract).then_inc(plo, 1)

            def keep(pair):
                after(pool, x2d, pair + 1)
                pool.tensor_copy(x2_all[:, bass.ds(pair * C, C)], x2_cur[:, :]).then_inc(x2c, 1)

            def queries(pair, s):
                after(pool, st_done, 2 * pair - 2)
                pool.tensor_copy(qk_cur[s][:, :, :], qk_all[:, :, bass.ds(pair * (2 * S), 2 * S)]).then_inc(qkc, 1)

            def steps(i):
                for s in range(2):
                    pair = 2 * i + s
                    n = 2 * pair
                    if not (isinstance(pair, int) and pair == NP - 1):
                        low_rows(n + 2, (2 * s + 2) % 4)
                        queries(pair + 1, 1 - s)
                        low_rows(n + 3, (2 * s + 3) % 4)
                    low_probs(n, 0)
                    low_probs(n + 1, 1)
                    if not (isinstance(pair, int) and pair == 0):
                        keep(pair - 1)

            low_rows(0, 0)
            low_rows(1, 1)
            pool.wait_ge(su_dve, 3 + NG)
            queries(0, 0)
            steps(0)
            with pool.Fori(1, NP // 2 - 1) as i:
                steps(i)
            steps(NP // 2 - 1)
            keep(NP - 1)

            def masks(i):
                after(pool, f_mo, i + 1)
                after(pool, f_a, i)
                pool.tensor_tensor(dm[:, :, :, :], chosen[:, NQ * HG:, :].unsqueeze(2).broadcast_to((P, NQ * HG, HALF, E)),
                                   diag_e[:, :, :].unsqueeze(1).broadcast_to((P, NQ * HG, HALF, E)), ALU.mult).then_inc(f_dm, 1)

            pool.wait_ge(c_dve, 11)
            pool.wait_ge(mvd, NP)
            masks(0)
            with pool.Fori(1, NP) as i:
                masks(i)

        @block.scalar
        def _(act):
            act.wait_ge(su_pe, SU_QV)
            act.copy(wqT[:, :], ps[:, 0, 0:P])
            act.copy(wvT[:, :], ps[:, 0, P:2 * P]).then_inc(su_act, 1)
            act.wait_ge(ln, 4)
            act.sqrt(st_std[:, :], st_ve[:, :]).then_inc(ln_sqrt, 1)
            act.wait_ge(su_pe, SU_G)
            for g in range(2):
                last = act.copy(wg[:, :, g, :, :].rearrange("p a b e -> p b a e"),
                                ps[:, 1, P * g:P * g + P].rearrange("p (b a e) -> p b a e", b=HG, a=4))
            last.then_inc(su_act, 1)
            act.wait_ge(su_pe, SU_V)
            act.copy(fwvT[:, :, :], ps[:, 2, :].rearrange("p (e d) -> p e d", e=E)).then_inc(su_act, 1)
            act.wait_ge(su_pe, SU_O)
            act.copy(wo2[:, :, :], ps[:, 3:5, :].rearrange("p a (e f) -> p (a e) f", f=C)).then_inc(su_act, 1)
            act.wait_ge(su_pe, SU_M)
            mT_v = mT[:, :, :].rearrange("p (a k h) c -> p h a k c", a=2, h=2)
            for n, (h2, a) in enumerate(((0, 0), (0, 1), (1, 0), (1, 1))):
                last = act.mul(mT_v[:, h2, a, :, :], ps[:, (5, 6, 7, 0)[n], :].rearrange("p (k c) -> p k c", c=C), SCALE)
            last.then_inc(su_act, 1)
            for g in range(NG):
                act.wait_ge(su_pe, SU_X + g)
                act.copy(xn1T[:, GW * g:GW * (g + 1)].rearrange("p (n t) -> p n t", t=S),
                         ps[:, 1 + g, :].rearrange("p (n t) -> p n t", t=SLOT)[:, :, 0:S]).then_inc(su_act, 1)
            for g in range(NG):
                act.wait_ge(su_pe, SU_X + NG + g)
                act.wait_ge(c_zero, 2)
                act.activation(qT[:, 8 * g:8 * g + 8, 0:S], ps[:, (5, 6, 7, 0)[g], 0:GW].rearrange("p (n t) -> p n t", t=S),
                               ACT.Identity, bias=bq_col[:, 0:1]).then_inc(su_act, 1)
            for g in range(NG):
                act.wait_ge(su_pe, SU_X + 2 * NG + g)
                act.copy(qk_all[:, 0, GW * g:GW * (g + 1)], ps[:, 1 + g, 0:GW]).then_inc(su_act, 1)

            def split_hi(n, k, turn):
                act.wait_ge(d_ctx[k], 48 * (turn + 1))
                after(act, pvd, n - 3)
                act.copy(nat[k][:, 0, :], ctxf[k][:, :]).then_inc(nathi, 1)

            def t_evac(n, b):
                after(act, tfull, 3 * n + 2)
                after(act, st_done, n - 1)
                act.copy(ctxT[b][:, 8 * P:16 * P], ps[:, (3 * b + 1) % 2, :].bitcast(F16)).then_inc(tev_a, 1)

            def exps(n, b):
                after(act, shd, n + 1)
                after(act, pvd, n - 1)
                act.activation(p16[:, 0, :, b, 0:S].rearrange("p (a t) q -> p a t q", a=2),
                               ps[:, 2 + 2 * b:4 + 2 * b, 0:6 * S].rearrange("p a (t q) -> p a t q", t=6), ACT.Exp).then_inc(expd, 1)
                act.activation(pf[b][:, :, :].rearrange("p (a t) q -> p a (t q)", a=2),
                               ps[:, 2 + 2 * b:4 + 2 * b, 0:6 * S], ACT.Exp).then_inc(expd, 1)

            def steps(i):
                for s in range(2):
                    pair = 2 * i + s
                    n = 2 * pair
                    more = not (isinstance(pair, int) and pair == NP - 1)
                    if more:
                        split_hi(n + 2, (2 * s + 2) % 4, i + s)
                        split_hi(n + 3, (2 * s + 3) % 4, i + s)
                    exps(n, 0)
                    if more:
                        t_evac(n + 2, 0)
                    exps(n + 1, 1)
                    if more:
                        t_evac(n + 3, 1)

            split_hi(0, 0, 0)
            split_hi(1, 1, 0)
            t_evac(0, 0)
            t_evac(1, 1)
            act.wait_ge(c_zero, 5)
            steps(0)
            with act.Fori(1, NP // 2 - 1) as i:
                steps(i)
            steps(NP // 2 - 1)

            act.wait_ge(l2a, 1)
            act.sqrt(st_std[:, :], st_ve[:, :]).then_inc(l2b, 1)

            def xnT_evac(i):
                after(act, f_xnT, i + 1)
                after(act, f_s, i)
                act.copy(xnT[:, 0:2 * S].rearrange("p (b t) -> p b t", b=2),
                         ps[:, 2, 0:P].rearrange("p (b t) -> p b t", b=2)[:, :, 0:S]).then_inc(f_xnTe, 1)

            def gates_out(i):
                after(act, f_g, i + 1)
                after(act, f_top, i)
                act.copy(g_sb[:, :, :].rearrange("p (g q n) e -> p q g (n e)", g=2, q=NQ),
                         ps[:, 2, 0:2 * P].rearrange("p (q g m) -> p q g m", q=NQ, g=2)).then_inc(f_ge, 1)
                act.wait_ge(f_ge, i + 1)
                after(act, f_sg, i)
                act.activation(th[:, :, :], g_sb[:, 0:16, :], ACT.Tanh, scale=0.5).then_inc(f_th, 1)

            def iteration(i, front=True, back=True, nxt=True):
                if back:
                    after(act, f_vt, i)
                    after(act, f_vv, i - 1)
                    act.copy(vT[:, :, :, 0:S].rearrange("p h b t -> p b t h"),
                             ps[:, 6:8, 0:8 * S].rearrange("p b (t h) -> p b t h", h=8)).then_inc(f_vte, 1)
                if front:
                    after(act, f_pj, i + 1)
                    after(act, f_vt, i)
                    act.copy(pj[:, :, :], ps[:, 3, :].rearrange("p (q d) -> p q d", d=DH)).then_inc(f_pje, 1)
                    after(act, f_z1, i + 1)
                    after(act, f_s, i)
                    act.copy(z[:, 0:8, :].rearrange("p (a k) n -> p a (k n)", a=2), ps[:, 0:2, 0:8 * S]).then_inc(f_z1e, 1)
                    after(act, f_tr, i + 1)
                    after(act, f_d, i)
                    act.copy(mixp[:, :, :], ps[:, 3, 0:P].rearrange("p (q h) -> p q h", h=H)).then_inc(f_tre, 1)
                if back:
                    after(act, f_vv, i)
                    after(act, f_pv, 2 * i - 2)
                    act.copy(v_sb[:, :, :].rearrange("p (a h) d -> p a (h d)", a=2), ps[:, 4:6, :]).then_inc(f_vve, 1)
                if front:
                    after(act, f_z2, i + 1)
                    after(act, f_s, i)
                    act.copy(z[:, 8:16, :].rearrange("p (a k) n -> p a (k n)", a=2), ps[:, 2:4, 0:8 * S]).then_inc(f_z2e, 1)
                if nxt:
                    xnT_evac(i + 1)
                if back:
                    after(act, f_a, i)
                    after(act, f_o, i - 1)
                    act.copy(aT[:, :, :, 0:S].rearrange("p e b t -> p b t e"),
                             ps[:, 4:6, 0:8 * S].rearrange("p b (t e) -> p b t e", e=E)).then_inc(f_ae, 1)
                if front:
                    after(act, f_sub, i + 1)
                    after(act, f_et, i)
                    after(act, f_rs, i)
                    act.activation(e_sb[:, :, :, 0:S].rearrange("p k b j -> p b k j"),
                                   ssub[:, :, :].rearrange("p (b k) j -> p b k j", b=2), ACT.Exp).then_inc(f_e, 1)
                if nxt:
                    gates_out(i + 1)
                if front:
                    after(act, f_et, i + 1)
                    after(act, f_pv, 2 * i)
                    act.copy(eT[:, :, :].rearrange("p (a k) n -> p a (k n)", a=2), ps[:, 0:2, :]).then_inc(f_ete, 1)

            act.wait_ge(c_zero, 22)
            xnT_evac(0)
            gates_out(0)
            iteration(0, back=False)
            iteration(1)
            with act.Fori(2, NP - 1) as i:
                iteration(i)
            iteration(NP - 1, nxt=False)
            iteration(NP, front=False, nxt=False)

        @block.vector
        def _(dve):
            v3 = lambda t: t[:, :].rearrange("p (n c) -> p n c", c=C)
            wide = lambda t: t[:, :].unsqueeze(2).broadcast_to((P, NP, C))
            dve.wait_ge(c_id, 2)
            dve.tensor_copy(ident16[:, :], ident[:, :]).then_inc(c_dve, 1)
            for b in range(2):
                dve.tensor_copy(diag_q[SLOT * b:SLOT * b + SLOT, :], ident[SLOT * b:SLOT * b + SLOT, SLOT * b:SLOT * b + S]).then_inc(c_dve, 1)
            dve.wait_ge(d_x, 32)
            dve.tensor_reduce(st_sum[:, :], v3(x_all), AX.X, ALU.add).then_inc(ln, 1)
            dve.wait_ge(ln, 1)
            dve.tensor_scalar(st_mean[:, :], st_sum[:, :], 1.0 / C, None, ALU.mult).then_inc(su_dve, 1)
            dve.wait_ge(su_dve, 1)
            dve.tensor_tensor(v3(y_all), v3(x_all), wide(st_mean), ALU.subtract).then_inc(ln, 1)
            dve.wait_ge(ln, 2)
            dve.tensor_tensor(x2_all[:, :], y_all[:, :], y_all[:, :], ALU.mult).then_inc(ln, 1)
            dve.wait_ge(ln, 3)
            dve.tensor_reduce(st_var[:, :], v3(x2_all), AX.X, ALU.add).then_inc(su_dve, 1)
            dve.wait_ge(su_dve, 2)
            dve.tensor_scalar(st_ve[:, :], st_var[:, :], 1.0 / C, EPS, ALU.mult, ALU.add).then_inc(ln, 1)
            dve.wait_ge(ln_sqrt, 1)
            dve.reciprocal(st_rstd[:, :], st_std[:, :]).then_inc(su_dve, 1)
            dve.wait_ge(su_dve, 3)
            dve.tensor_tensor(v3(y_all), v3(y_all), wide(st_rstd), ALU.mult).then_inc(ln, 1)
            dve.wait_ge(d_w, 16 * NW)
            dve.tensor_tensor(v3(x_all), v3(x_all), bv_all[:, :].unsqueeze(1).broadcast_to((P, NP, C)), ALU.add).then_inc(ln, 1)
            for q in range(4):
                r = slice(32 * q, 32 * q + 32)
                cut = ident[r, 32 * q:32 * q + HALF].unsqueeze(2)
                dve.tensor_copy(diag_h[r, :, :], cut.broadcast_to((32, HALF, H))).then_inc(c_dve, 1)
                dve.tensor_copy(diag_e[r, :, :], cut.broadcast_to((32, HALF, E))).then_inc(c_dve, 1)
            for g in range(NG):
                dve.wait_ge(su_act, SU_X + 2 * NG + g)
                dve.tensor_tensor(qk_all[:, 1, GW * g:GW * (g + 1)], ps[:, 1 + g, 0:GW],
                                  qk_all[:, 0, GW * g:GW * (g + 1)], ALU.subtract).then_inc(su_dve, 1)
            dve.wait_ge(su_pe, SU_X + 3 * NG)
            dve.tensor_copy(cq[:, :], ps[:, 5, 0:NP]).then_inc(su_dve, 1)

            def split_lo(n, k):
                after(dve, nathi, n + 1)
                dve.tensor_tensor(nat[k][:, 1, 0:8 * C], ctxf[k][:, 0:8 * C], nat[k][:, 0, 0:8 * C],
                                  ALU.subtract).then_inc(natlo, 1)

            def t_evac(n, b, c):
                after(dve, tfull, 3 * n + c + 1)
                after(dve, st_done, n - 1)
                dve.tensor_copy(ctxT[b][:, 8 * P * c:8 * P * (c + 1)], ps[:, (3 * b + c) % 2, :].bitcast(F16)).then_inc(tev_d, 1)

            def tile_max(n, pair, b):
                after(dve, st_done, n + 1)
                after(dve, tmT, pair)
                dve.tensor_reduce(tmax[:, b, 0:S], ps[:, 2 + 2 * b:4 + 2 * b, 0:6 * S].rearrange("p a (t q) -> p q a t", t=6),
                                  AX.XY, ALU.max).then_inc(tmx, 1)

            def shifts(pair):
                after(dve, tmT, pair + 1)
                dve.tensor_reduce(m_q[:, :], ps[:, 7, 0:P], AX.X, ALU.max).then_inc(mred, 1)
                dve.wait_ge(mred, pair + 1)
                dve.scalar_tensor_tensor(nshift[:, :], m_q[:, :], cq[:, bass.ds(pair, 1)], cq[:, bass.ds(pair, 1)],
                                         op0=ALU.add, op1=ALU.subtract).then_inc(nsh, 1)
                dve.wait_ge(nsh, pair + 1)
                after(dve, shd, 2 * pair)
                dve.tensor_scalar(dg[:, 0, :], diag_q[:, :], nshift[:, 0:1], None, ALU.mult).then_inc(dghi, 1)
                dve.wait_ge(dghi, pair + 1)
                dve.scalar_tensor_tensor(dg[:, 1, :], diag_q[:, :], nshift[:, 0:1], dg[:, 0, :],
                                         op0=ALU.mult, op1=ALU.subtract).then_inc(dgr, 1)

            def sums_out(pair):
                after(dve, pvd, 2 * pair + 2)
                after(dve, prj, pair)
                dve.tensor_copy(aoT[:, :, 0:S], ps[:, 6, 0:P].rearrange("p (b q) -> p b q", b=2)[:, :, 0:S]).then_inc(aor, 1)
                dve.reciprocal(rden[:, :], ps[:, 6, P:P + 1]).then_inc(rdn, 1)

            def result(pair):
                after(dve, rdn, pair + 1)
                after(dve, x2c, pair)
                after(dve, prj, pair + 1)
                dve.scalar_tensor_tensor(x2_cur[:, :], ps[:, 6, 2 * P:3 * P], rden[:, 0:1],
                                         x_all[:, bass.ds(pair * C, C)], op0=ALU.mult, op1=ALU.add).then_inc(x2d, 1)
                dve.wait_ge(x2d, pair + 1)
                dve.bn_stats(bst[:, :], x2_cur[:, :]).then_inc(bsd, 1)
                dve.wait_ge(c_zero, 6)
                dve.wait_ge(bsd, pair + 1)
                dve.bn_aggr(mv_cur[:, :], bst[:, :]).then_inc(mvc, 1)
                dve.wait_ge(mvc, pair + 1)
                dve.tensor_copy(mv_all[:, bass.ds(pair * 2, 2)], mv_cur[:, :]).then_inc(mvd, 1)

            def steps(i):
                for s in range(2):
                    pair = 2 * i + s
                    n = 2 * pair
                    first = isinstance(pair, int) and pair == 0
                    more = not (isinstance(pair, int) and pair == NP - 1)
                    tile_max(n, pair, 0)
                    tile_max(n + 1, pair, 1)
                    shifts(pair)
                    if more:
                        split_lo(n + 2, (2 * s + 2) % 4)
                    if not first:
                        sums_out(pair - 1)
                    if more:
                        split_lo(n + 3, (2 * s + 3) % 4)
                        t_evac(n + 2, 0, 0)
                        t_evac(n + 2, 0, 2)
                        t_evac(n + 3, 1, 0)
                    if not first:
                        result(pair - 1)
                    if more:
                        t_evac(n + 3, 1, 2)

            for b in range(2):
                split_lo(b, b)
            for b in range(2):
                t_evac(b, b, 0)
                t_evac(b, b, 2)
            dve.wait_ge(c_zero, 6)
            steps(0)
            with dve.Fori(1, NP // 2 - 1) as i:
                steps(i)
            steps(NP // 2 - 1)
            sums_out(NP - 1)
            result(NP - 1)

            dve.wait_ge(mvd, NP)
            dve.tensor_scalar(st_ve[:, :], mv_all[:, :].rearrange("p (n k) -> p n k", k=2)[:, :, 1], EPS, None, ALU.add).then_inc(l2a, 1)
            dve.wait_ge(l2b, 1)
            dve.reciprocal(st_rstd[:, :], st_std[:, :]).then_inc(l2c, 1)
            dve.wait_ge(l2c, 1)

            def normalise(i):
                after(dve, f_xnT, i)
                dve.tensor_scalar(xn[:, :], x2_all[:, bass.ds(i * C, C)], mv_all[:, bass.ds(i * 2, 1)],
                                  st_rstd[:, bass.ds(i, 1)], ALU.subtract, ALU.mult).then_inc(f_xn, 1)

            per8 = lambda t: t[:, :].unsqueeze(2).broadcast_to((P, 32, E))

            def top_two(i):
                after(dve, f_ge, i + 1)
                dve.tensor_reduce(m1[:, :], g_sb[:, :, :], AX.X, ALU.max).then_inc(t_[0], 1)
                dve.wait_ge(t_[0], i + 1)
                dve.tensor_tensor(eq1[:, :, :], g_sb[:, :, :], per8(m1), ALU.is_equal).then_inc(t_[1], 1)
                dve.wait_ge(t_[1], i + 1)
                dve.tensor_tensor(r1[:, :, :], eq1[:, :, :], rank[:, :, :], ALU.mult).then_inc(t_[2], 1)
                dve.wait_ge(t_[2], i + 1)
                dve.tensor_reduce(s1[:, :], r1[:, :, :], AX.X, ALU.max).then_inc(t_[3], 1)
                dve.wait_ge(t_[3], i + 1)
                dve.tensor_tensor(oh1[:, :, :], r1[:, :, :], per8(s1), ALU.is_equal).then_inc(t_[4], 1)
                dve.wait_ge(t_[4], i + 1)
                dve.scalar_tensor_tensor(g2[:, :, :], oh1[:, :, :], -3.0e38, g_sb[:, :, :], op0=ALU.mult, op1=ALU.add).then_inc(f_top, 1)
                dve.wait_ge(f_top, i + 1)
                dve.tensor_reduce(m2[:, :], g2[:, :, :], AX.X, ALU.max).then_inc(t_[5], 1)
                dve.wait_ge(t_[5], i + 1)
                dve.tensor_tensor(eq2[:, :, :], g2[:, :, :], per8(m2), ALU.is_equal).then_inc(t_[6], 1)
                dve.wait_ge(t_[6], i + 1)
                dve.tensor_tensor(r2[:, :, :], eq2[:, :, :], rank[:, :, :], ALU.mult).then_inc(t_[7], 1)
                dve.wait_ge(t_[7], i + 1)
                dve.tensor_reduce(s2[:, :], r2[:, :, :], AX.X, ALU.max).then_inc(t_[8], 1)
                dve.wait_ge(t_[8], i + 1)
                dve.tensor_tensor(oh2[:, :, :], r2[:, :, :], per8(s2), ALU.is_equal).then_inc(t_[9], 1)
                dve.wait_ge(t_[9], i + 1)
                after(dve, f_dm, i)
                dve.tensor_tensor(chosen[:, :, :], oh1[:, :, :], oh2[:, :, :], ALU.add).then_inc(f_mo, 1)

            def mixing(i):
                after(dve, f_th, i + 1)
                dve.tensor_scalar(sg[:, :, :], th[:, :, :], 0.5, 0.5, ALU.mult, ALU.add).then_inc(f_sg, 1)
                dve.wait_ge(f_sg, i + 1)
                dve.wait_ge(f_mo, i + 1)
                after(dve, f_tr, i)
                dve.tensor_tensor(mix[:, :, :, :].rearrange("p q n e -> p (q n) e"), sg[:, :, :], chosen[:, 0:NQ * HG, :],
                                  ALU.mult).then_inc(f_mix, 1)

            def iteration(i, front=True, back=True, nxt=True):
                if front:
                    mixing(i)
                if nxt:
                    normalise(i + 1)
                if front:
                    after(dve, f_tre, i + 1)
                    after(dve, f_vt, i)
                    dve.tensor_tensor(dv[:, :, :, :],
                                      mixp[:, :, :].unsqueeze(2).broadcast_to((P, 2 * NQ, HALF, H)),
                                      diag_h[:, :, :].unsqueeze(1).broadcast_to((P, 2 * NQ, HALF, H)), ALU.mult).then_inc(f_d, 1)
                if back:
                    after(dve, f_ri, i)
                    after(dve, f_a, i - 1)
                    for b in range(2):
                        k = slice(K16 * b, K16 * b + K16)
                        after(dve, f_pv, 2 * i - 1 + b)
                        dve.tensor_tensor(attnf[:, k, :], ps[:, 6 + b, :].rearrange("p (k d) -> p k d", d=DH),
                                          rinv[:, :].rearrange("p (k b) -> p b k", b=2)[:, b, :].unsqueeze(2).broadcast_to((P, K16, DH)),
                                          ALU.mult).then_inc(f_nrm, 1)
                        dve.wait_ge(f_nrm, 2 * i - 1 + b)
                        dve.tensor_copy(ah[:, k, 0, :], attnf[:, k, :]).then_inc(f_ahi, 1)
                        dve.wait_ge(f_ahi, 2 * i - 1 + b)
                        dve.tensor_tensor(ah[:, k, 1, :], attnf[:, k, :], ah[:, k, 0, :], ALU.subtract).then_inc(f_alo, 1)
                if front:
                    after(dve, f_s, i + 1)
                    dve.tensor_reduce(smx[:, :], ps[:, 0:2, 0:8 * S].rearrange("p b (k j) -> p b k j", j=S), AX.X, ALU.max).then_inc(f_mx, 1)
                    dve.wait_ge(f_mx, i + 1)
                    after(dve, f_e, i)
                    dve.tensor_tensor(ssub[:, :, :].rearrange("p (b k) j -> p b k j", b=2),
                                      ps[:, 0:2, 0:8 * S].rearrange("p b (k j) -> p b k j", j=S),
                                      smx[:, :].rearrange("p (b k) -> p b k", b=2).unsqueeze(3).broadcast_to((P, 2, K16, S)),
                                      ALU.subtract).then_inc(f_sub, 1)
                    after(dve, f_e, i + 1)
                    dve.tensor_reduce(rs[:, :], e_sb[:, :, :, :].rearrange("p k b j -> p (k b) j"), AX.X, ALU.add).then_inc(f_rs, 1)
                    dve.wait_ge(f_rs, i + 1)
                    dve.reciprocal(rinv[:, :], rs[:, :]).then_inc(f_ri, 1)
                if back:
                    after(dve, f_o, i)
                    dve.tensor_tensor(y_all[:, bass.ds((i - 1) * C, C)], ps[:, 3, 0:C], x2_all[:, bass.ds((i - 1) * C, C)],
                                      ALU.add).then_inc(f_y, 1)
                if nxt:
                    top_two(i + 1)

            dve.wait_ge(c_zero, 22)
            dve.wait_ge(x2c, NP)
            normalise(0)
            top_two(0)
            iteration(0, back=False)
            iteration(1)
            with dve.Fori(2, NP - 1) as i:
                iteration(i)
            iteration(NP - 1, nxt=False)
            iteration(NP, front=False, nxt=False)

        @block.tensor
        def _(pe):
            pe.wait_ge(c_id, 2)
            pe.wait_ge(d_w, 16 * NW)
            pe.transpose(ps[:, 0, 0:P], wq_nat[:, :], ident[:, :])
            pe.transpose(ps[:, 0, P:2 * P], wv_nat[:, :], ident[:, :]).then_inc(su_pe, 1)
            pe.wait_ge(d_fw, 16 * NFW)
            pe.transpose(ps[:, 1, 0:P], fws_nat[:, :], ident[:, :])
            pe.transpose(ps[:, 1, P:2 * P], fwd_nat[:, :], ident[:, :]).then_inc(su_pe, 1)
            for k in range(E // 2):
                last = pe.transpose(ps[:, 2, P * k:P * k + P], fwv_nat[:, k, :], ident[:, :])
            last.then_inc(su_pe, 1)
            for e in range(E):
                last = pe.transpose(ps[:, 3 + e // 4, P * (e % 4):P * (e % 4) + P], fwo_nat[:, e, :, :].rearrange("p a d -> p (a d)"), ident[:, :])
            last.then_inc(su_pe, 1)
            pe.wait_ge(su_act, 1)
            for n, (h2, a) in enumerate(((0, 0), (0, 1), (1, 0), (1, 1))):
                for k in range(4):
                    last = pe.matmul(ps[:, (5, 6, 7, 0)[n], P * k:P * k + P], fwk_nat[DH * h2:DH * h2 + DH, 4 * a + k, :],
                                     fwq_nat[DH * h2:DH * h2 + DH, 4 * a + k, :], start=True, stop=True)
            last.then_inc(su_pe, 1)
            pe.wait_ge(ln, 5)
            for g in range(NG):
                pe.wait_ge(su_act, 4)
                for k in range(4):
                    n = 4 * g + k
                    last = pe.transpose(ps[:, 1 + g, P * k:P * k + P], y_all[:, C * n:C * n + C], ident[:, :])
                last.then_inc(su_pe, 1)
            for g in range(NG):
                pe.wait_ge(su_act, 5 + g + 1)
                pe.matmul(ps[:, (5, 6, 7, 0)[g], 0:GW], wqT[:, :], xn1T[:, GW * g:GW * (g + 1)], start=True, stop=True).then_inc(su_pe, 1)
            for g in range(NG):
                pe.wait_ge(su_act, 5 + NG + g + 1)
                pe.matmul(ps[:, 1 + g, 0:GW], wk_nat[:, :], qT[:, 8 * g:8 * g + 8, 0:S], start=True, stop=True).then_inc(su_pe, 1)
            for n in range(NP):
                last = pe.matmul(ps[:, 5, n:n + 1], qT[:, 2 * n:2 * n + 2, :].rearrange("p b t -> p (b t)"), bk_col[:, :], start=True, stop=True)
            last.then_inc(su_pe, 1)
            pe.wait_ge(su_act, 5 + 3 * NG)
            pe.wait_ge(su_dve, 3 + NG + 1)
            pe.wait_ge(c_dve, 3)
            pe.wait_ge(c_zero, 10)

            def turn(n, b, k):
                after(pe, nathi, n + 1)
                after(pe, natlo, n + 1)
                after(pe, natlo2, n + 1)
                for c in range(3):
                    if c == 0:
                        after(pe, tev_a, n)
                    elif c == 1:
                        after(pe, tev_d, 2 * n)
                    else:
                        after(pe, tev_d, 2 * n + 1)
                    for j in range(8 * c, 8 * c + 8):
                        last = pe.transpose(ps[:, (3 * b + c) % 2, :].bitcast(F16)[:, P * (j % 8):P * (j % 8) + P],
                                            nat[k][:, j // TK, C * (j % TK):C * (j % TK) + C], ident16[:, :])
                    last.then_inc(tfull, 1)

            def scores(n, pair, s, b):
                after(pe, tev_d, 2 * n + 2)
                after(pe, tev_a, n + 1)
                after(pe, qkc, pair + 1)
                after(pe, expd, 2 * n - 2)
                for t in range(TK):
                    o = ps[:, 2 + 2 * b + t // 6, S * (t % 6):S * (t % 6) + S]
                    hi = ctxT[b][:, P * t:P * t + P]
                    lo = ctxT[b][:, P * (TK + t):P * (TK + t) + P]
                    qh, ql = qk_cur[s][:, 0, S * b:S * b + S], qk_cur[s][:, 1, S * b:S * b + S]
                    pe.matmul(o, hi, qh, start=(t % 6 == 0), stop=False, skip_group_check=True)
                    pe.matmul(o, hi, ql, start=False, stop=False, skip_group_check=True)
                    last = pe.matmul(o, lo, qh, start=False, stop=False, skip_group_check=True)
                last.then_inc(st_done, 1)

            def max_turn(pair):
                after(pe, tmx, 2 * pair + 2)
                after(pe, mred, pair)
                pe.transpose(ps[:, 7, 0:P], tmax[:, :, :].rearrange("p b q -> p (b q)"), ident[:, :]).then_inc(tmT, 1)

            def shift(n, pair, b):
                after(pe, dgr, pair + 1)
                for a in range(2):
                    o = ps[:, 2 + 2 * b + a, 0:6 * S].rearrange("p (t q) -> p t q", t=6)
                    for part in range(2):
                        last = pe.matmul(o, rows_of[:, b, :],
                                         dg[:, part, :].unsqueeze(1).broadcast_to((P, 6, S)),
                                         start=False, stop=(part == 1), skip_group_check=True)
                last.then_inc(shd, 1)

            def values(n, pair, b, k):
                after(pe, plo, n + 1)
                if b == 0:
                    after(pe, x2d, pair)
                o = ps[:, 6, SLOT * b:SLOT * b + S]
                for t in range(TK):
                    r = slice(0, P if t < TK - 1 else REST)
                    hi, lo = nat[k][r, 0, C * t:C * t + C], nat[k][r, 1, C * t:C * t + C]
                    ph, pl = p16[r, 0, t, b, 0:S], p16[r, 1, t, b, 0:S]
                    pe.matmul(o, hi, ph, start=(t == 0), stop=False)
                    pe.matmul(o, hi, pl, start=False, stop=False)
                    last = pe.matmul(o, lo, ph, start=False, stop=(t == TK - 1))
                if b == 1:
                    for part in range(2):
                        for t in range(TK):
                            r = slice(0, P if t < TK - 1 else REST)
                            last = pe.matmul(ps[:, 6, P:P + 1], p16[r, part, t, :, :].rearrange("p b q -> p (b q)"), ones16[r, :],
                                             start=(part == 0 and t == 0), stop=(part == 1 and t == TK - 1))
                last.then_inc(pvd, 1)

            def project(pair):
                after(pe, aor, pair + 1)
                after(pe, rdn, pair + 1)
                pe.matmul(ps[:, 6, 2 * P:3 * P], aoT[:, :, :].rearrange("p b q -> p (b q)"), wvT[:, :], start=True, stop=True).then_inc(prj, 1)

            def steps(i):
                for s in range(2):
                    pair = 2 * i + s
                    n = 2 * pair
                    first = isinstance(pair, int) and pair == 0
                    more = not (isinstance(pair, int) and pair == NP - 1)
                    k0, k1 = (2 * s + 2) % 4, (2 * s + 3) % 4
                    scores(n, pair, s, 0)
                    scores(n + 1, pair, s, 1)
                    if not first:
                        values(n - 2, pair - 1, 0, k0)
                    max_turn(pair)
                    if not first:
                        values(n - 1, pair - 1, 1, k1)
                    shift(n, pair, 0)
                    shift(n + 1, pair, 1)
                    if more:
                        turn(n + 2, 0, k0)
                    if not first:
                        project(pair - 1)
                    if more:
                        turn(n + 3, 1, k1)

            for b in range(2):
                turn(b, b, b)
            steps(0)
            with pe.Fori(1, NP // 2 - 1) as i:
                steps(i)
            steps(NP // 2 - 1)
            for b in range(2):
                values(2 * NP - 2 + b, NP - 1, b, 2 + b)
            project(NP - 1)

            def xn_turn(i):
                after(pe, f_xn, i + 1)
                after(pe, f_z2e, i)
                pe.transpose(ps[:, 2, 0:P], xn[:, :], ident[:, :]).then_inc(f_xnT, 1)

            def z_heads(h0, first_bank):
                for h in range(h0, h0 + 8):
                    k = h - h0
                    last = pe.matmul(ps[:, first_bank + k // 4, 2 * S * (k % 4):2 * S * (k % 4) + 2 * S], mT[:, h, :], xnT[:, 0:2 * S],
                                     start=True, stop=True)
                return last

            def gates(i):
                after(pe, f_xnTe, i + 1)
                for q in range(NQ):
                    for h4 in range(4):
                        last = pe.matmul(ps[32 * h4:32 * h4 + 32, 2, 64 * q:64 * q + 64], xnT[:, HALF * q:HALF * q + 32],
                                         wg[:, h4, :, :, :].rearrange("p g n e -> p (g n e)"), start=True, stop=True)
                last.then_inc(f_g, 1)

            def iteration(i, front=True, back=True, nxt=True):
                if back:
                    after(pe, f_d, i)
                    after(pe, f_pje, i)
                    after(pe, f_nrm, 2 * i - 2)
                    for q in range(NQ):
                        for par in range(2):
                            o = ps[DH * par:DH * par + DH, 6 + q // 2, 224 * (q % 2):224 * (q % 2) + 224].rearrange("p (t h) -> p t h", h=8)
                            for eg in range(2):
                                last = pe.matmul(o, pj[:, 2 * q + eg, :], dv[:, 2 * q + eg, :, 8 * par:8 * par + 8],
                                                 start=(eg == 0), stop=(eg == 1))
                    last.then_inc(f_vt, 1)
                if front:
                    after(pe, f_y, i - 1)
                    for q in range(NQ):
                        for e4 in range(4):
                            last = pe.matmul(ps[32 * e4:32 * e4 + 32, 3, P * q:P * q + P].rearrange("p (a d) -> p a d", a=2),
                                             xnT[:, HALF * q:HALF * q + 32],
                                             fwvT[:, e4::4, :], start=True, stop=True)
                    last.then_inc(f_pj, 1)
                    after(pe, f_ete, i)
                    z_heads(0, 0).then_inc(f_z1, 1)
                    after(pe, f_mix, i + 1)
                    after(pe, f_pje, i + 1)
                    for h4 in range(4):
                        for e4 in range(4):
                            o = ps[32 * e4:32 * e4 + 32, 3, 0:P].rearrange("p (q a h) -> p q a h", q=NQ, a=2)
                            first = 8 * (h4 % 2) + h4 // 2
                            last = pe.matmul(o[:, :, :, first:first + 7:2], ident[:, 32 * h4:32 * h4 + 32],
                                             mix[:, :, :, e4::4].rearrange("p q n a -> p q a n"), start=True, stop=True)
                    last.then_inc(f_tr, 1)
                if back:
                    after(pe, f_vte, i)
                    after(pe, f_ae, i - 1)
                    for k in range(8):
                        last = pe.transpose(ps[:, 4 + k // 4, P * (k % 4):P * (k % 4) + P],
                                            vT[:, k, :, :].rearrange("p b t -> p (b t)"), ident[:, :])
                    last.then_inc(f_vv, 1)
                if front:
                    after(pe, f_ge, i + 1)
                    after(pe, f_tre, i + 1)
                    z_heads(8, 2).then_inc(f_z2, 1)
                if back:
                    pe.wait_ge(mvd, NP)
                    after(pe, f_ete, i)
                    after(pe, f_vve, i)
                    for b in range(2):
                        for half in range(2):
                            for hg in range(HG):
                                for h4 in range(4):
                                    last = pe.matmul(ps[32 * h4:32 * h4 + 32, 6 + b, 256 * half + 64 * hg:256 * half + 64 * hg + 64],
                                                     eT[SLOT * b:SLOT * b + SLOT, HG * half + hg, 32 * h4:32 * h4 + 32],
                                                     v_sb[SLOT * b:SLOT * b + SLOT, 4 * hg + h4, :], start=True, stop=True)
                        last.then_inc(f_pv, 1)
                if front:
                    after(pe, f_z1e, i + 1)
                    after(pe, f_z2e, i + 1)
                    for q in range(NQ):
                        b = q // 2
                        for h4 in range(4):
                            last = pe.matmul(ps[32 * h4:32 * h4 + 32, b, 224 * (q % 2):224 * (q % 2) + 224].rearrange("p (n j) -> p n j", j=S),
                                             xnT[:, HALF * q:HALF * q + 32], z[:, h4::4, S * b:S * b + S], start=True, stop=True)
                    last.then_inc(f_s, 1)
                if nxt:
                    xn_turn(i + 1)
                if back:
                    after(pe, f_dm, i)
                    for q in range(NQ):
                        if q % 2 == 0:
                            after(pe, f_alo, 2 * i - 1 + q // 2)
                        for hg in range(HG):
                            n = HG * q + hg
                            last = pe.matmul(ps[:, 4 + q // 2, 224 * (q % 2):224 * (q % 2) + 224], ah[:, n, :, :].rearrange("p a d -> p (a d)"),
                                             dm[:, n, :, :].rearrange("p t e -> p (t e)"), start=(hg == 0), stop=(hg == HG - 1))
                    last.then_inc(f_a, 1)
                if nxt:
                    gates(i + 1)
                if back:
                    after(pe, f_ae, i)
                    if front:
                        after(pe, f_z2e, i + 1)
                    for e in range(E):
                        last = pe.matmul(ps[:, 3, 0:C], aT[:, e, :, :].rearrange("p b t -> p (b t)"), wo2[:, e, :],
                                         start=(e == 0), stop=(e == E - 1))
                    last.then_inc(f_o, 1)
                if front:
                    after(pe, f_e, i + 1)
                    after(pe, f_sub, i + 1)
                    for k in range(K16):
                        last = pe.transpose(ps[:, k // 4, P * (k % 4):P * (k % 4) + P],
                                            e_sb[:, k, :, :].rearrange("p b j -> p (b j)"), ident[:, :])
                    last.then_inc(f_et, 1)

            pe.wait_ge(mvd, NP)
            xn_turn(0)
            gates(0)
            iteration(0, back=False)
            iteration(1)
            with pe.Fori(2, NP - 1) as i:
                iteration(i)
            iteration(NP - 1, nxt=False)
            iteration(NP, front=False, nxt=False)


_INS = ['x', 'ctx_1024', 'L0_xattn_Wq', 'L0_xattn_bq', 'L0_xattn_Wk', 'L0_xattn_bk', 'L0_xattn_Wv', 'L0_xattn_bv',
        'L0_ffn_Wq', 'L0_ffn_Wk', 'L0_ffn_Wv', 'L0_ffn_Ws', 'L0_ffn_Wd', 'L0_ffn_Wo']
_OUTS = [((32, 56, 128), 'float32')]


def kernel(**inputs):
    import numpy as _np
    import concourse.bacc as _bacc
    from concourse import mybir as _mybir
    from concourse.bass_utils import run_bass_kernel_spmd as _run

    nc = _bacc.Bacc("TRN2", target_bir_lowering=False, num_devices=1)
    arrays, args = {}, []
    for name in _INS:
        a = _np.ascontiguousarray(inputs[name])
        arrays[f"in_{name}_dram"] = a
        args.append(nc.dram_tensor(f"in_{name}_dram", a.shape, _mybir.dt.from_np(a.dtype), kind="ExternalInput").ap())
    for i, (shape, dtype) in enumerate(_OUTS):
        dt = _mybir.dt.from_np(_np.dtype(dtype))
        args.append(nc.dram_tensor(f"out_{i}_dram", shape, dt, kind="ExternalOutput").ap())
    xattn_ffn(nc, *args)
    r = _run(nc, [arrays], core_ids=[0])
    return r.results[0]["out_0_dram"]
```

```python
from contextlib import ExitStack

import concourse.bass as bass
from concourse import mybir

F32 = mybir.dt.float32
F16 = mybir.dt.float16
BF16 = mybir.dt.bfloat16
ALU = mybir.AluOpType
ACT = mybir.ActivationFunctionType
AX = mybir.AxisListType

P = 128
BANK = 512


def xattn_ffn(
    nc: bass.Bass,
    x: bass.AP,
    ctx: bass.AP,
    wq: bass.AP,
    bq: bass.AP,
    wk: bass.AP,
    bk: bass.AP,
    wv: bass.AP,
    bv: bass.AP,
    fwq: bass.AP,
    fwk: bass.AP,
    fwv: bass.AP,
    fws: bass.AP,
    fwd: bass.AP,
    fwo: bass.AP,
    out: bass.AP,
):
    B, S, C = x.shape
    L = ctx.shape[1]
    H, DH, _ = fwq.shape
    E = fwv.shape[0]
    assert C == P and S == 56 and H == 16 and DH == 64 and E == 8
    NP = B // 2
    SLOT = 64
    HALF = S // 2
    TK = -(-L // P)
    RPP = L // P
    REST = L - RPP * P
    DUP = P - REST
    EPS = 1e-5
    SCALE = float(DH) ** -0.5
    HG = H // 4
    NQ = 4
    K16 = 2 * HG
    MIX_UP, PJ_UP = 4096.0, 16.0
    DVE_K = 5

    x_v = x.rearrange("(p b) t c -> b t p c", b=2)
    out_v = out.rearrange("(p b) t c -> b t p c", b=2)

    es = ExitStack()
    with es:
        def sb(name, shape, dt=F32):
            return es.enter_context(nc.sbuf_tensor(name, shape, dt))

        def sem(name):
            return es.enter_context(nc.semaphore(name))

        ps = es.enter_context(nc.psum_tensor("ps", [P, 8, BANK], F32))

        ident = sb("ident", [P, P])
        ident16 = sb("ident16", [P, P], F16)
        diag_q = sb("diag_q", [P, S])
        ones16 = sb("ones16", [P, 1], F16)
        rows_of = sb("rows_of", [P, 2, P], BF16)
        diag_h = sb("diag_h", [P, HALF, H], F16)
        diag_e = sb("diag_e", [P, HALF, E], F16)
        rank = sb("rank", [P, 32, E], F16)

        x_all = sb("x_all", [P, NP * C])
        x2_all = sb("x2_all", [P, NP * C])
        y_all = sb("y_all", [P, NP * C])
        bv_all = sb("bv_all", [P, C])
        bq_col = sb("bq_col", [P, 1])
        bk_col = sb("bk_col", [P, 1])
        st_ve = sb("st_ve", [P, NP])
        st_std = sb("st_std", [P, NP])
        st_rstd = sb("st_rstd", [P, NP])

        wq_nat = sb("wq_nat", [P, C])
        wk_nat = sb("wk_nat", [P, C])
        wv_nat = sb("wv_nat", [P, C])
        wqT = sb("wqT", [P, C])
        wvT = sb("wvT", [P, C])
        xn1T = sb("xn1T", [P, B * S])
        qT = sb("qT", [P, B, SLOT])
        qk_all = sb("qk_all", [P, 2, B * S], F16)
        bk_rep = sb("bk_rep", [P, C])
        bkq = sb("bkq", [P, C + 1])
        cq_x = sb("cq_x", [P, NP])
        cq = sb("cq", [P, NP])

        ctxf_all = sb("ctxf_all", [P, 4 * TK * C])
        ctxf = [ctxf_all[:, TK * C * k:TK * C * (k + 1)] for k in range(4)]
        nat = [sb(f"nat{k}", [P, 2, TK * C], F16) for k in range(4)]
        ctxT = [sb(f"ctxT{b}", [P, 2 * TK * P], F16) for b in range(2)]
        qk_cur = [sb(f"qk_cur{s}", [P, 2, 2 * S], F16) for s in range(2)]
        tmax = sb("tmax", [P, 2, SLOT])
        m_q = sb("m_q", [P, 1])
        nshift = sb("nshift", [P, 1])
        dg = sb("dg", [P, 2, S], BF16)
        pf = [sb(f"pf{b}", [P, TK, S]) for b in range(2)]
        p16 = sb("p16", [P, 2, TK, 2, SLOT], F16)
        rden = sb("rden", [P, 1])
        aoT = sb("aoT", [P, 2, SLOT])
        bst = sb("bst", [P, 6])
        bst_all = sb("bst_all", [P, NP, 6])
        mv_all = sb("mv_all", [P, NP * 2])
        mv_cur = sb("mv_cur", [P, 2])
        x2_cur = sb("x2_cur", [P, C])

        fwq_nat = sb("fwq_nat", [P, H // 2, C])
        fwk_nat = sb("fwk_nat", [P, H // 2, C])
        fwv_nat = sb("fwv_nat", [P, E // 2, C])
        fws_nat = sb("fws_nat", [P, C])
        fwd_nat = sb("fwd_nat", [P, C])
        fwo_nat = sb("fwo_nat", [P, E, 2, DH])
        mT = sb("mT", [P, 2, H, C], F16)
        wg = sb("wg", [P, 4, 2, HG, E])
        fwvT = sb("fwvT", [P, E, DH])
        wo2 = sb("wo2", [P, E, C])

        xn = sb("xn", [P, C])
        xnT = sb("xnT", [P, 2 * S + 4])
        xn16 = sb("xn16", [P, 2, 2 * S], F16)
        z = xn1T[:, :].rearrange("p (h n) -> p h n", h=H)
        g_sb = sb("g_sb", [P, 32, E])
        th = sb("th", [P, NQ * HG, E])
        sg = sb("sg", [P, NQ * HG, E])
        m1 = sb("m1", [P, 32])
        eq1 = sb("eq1", [P, 32, E], F16)
        r1 = sb("r1", [P, 32, E], F16)
        s1 = sb("s1", [P, 32], F16)
        oh1 = sb("oh1", [P, 32, E], F16)
        g2 = sb("g2", [P, 32, E])
        m2 = sb("m2", [P, 32])
        eq2 = sb("eq2", [P, 32, E], F16)
        r2 = sb("r2", [P, 32, E], F16)
        s2 = sb("s2", [P, 32], F16)
        oh2 = sb("oh2", [P, 32, E], F16)
        chosen = sb("chosen", [P, 2 * NQ * HG, E], F16)
        mix = sb("mix", [P, NQ, HG, E])
        mixf = sb("mixf", [P, NQ * 2, H])
        mixp = sb("mixp", [P, 2, NQ * 2, H], F16)
        n_dv, n_dm, n_pj = NQ * 2 * HALF * H, NQ * HG * HALF * E // 2, NQ * 2 * DH
        assert n_dv + n_dm + n_pj <= 4 * TK * C
        dv = ctxf_all[:, 0:n_dv].bitcast(F16).rearrange("p (s k t h) -> p s k t h", s=2, k=NQ * 2, h=H)
        dm = ctxf_all[:, n_dv:n_dv + n_dm].bitcast(F16).rearrange("p (k t e) -> p k t e", k=NQ * HG, e=E)
        pj = ctxf_all[:, n_dv + n_dm:n_dv + n_dm + n_pj].bitcast(F16).rearrange("p (s k d) -> p s k d", s=2, d=DH)
        pjf = sb("pjf", [P, NQ * 2, DH])
        smx = sb("smx", [P, 2 * K16])
        ssub = sb("ssub", [P, 2 * K16, S])
        e_sb = sb("e_sb", [P, K16, 2, SLOT])
        rs = sb("rs", [P, K16 * 2])
        rinv = sb("rinv", [P, K16 * 2])
        eT = sb("eT", [P, 2, K16, P])
        vT = sb("vT", [P, H // 2, 2, SLOT])
        v_sb = sb("v_sb", [P, H, DH])
        attnf = sb("attnf", [P, 2 * K16, DH])
        ah = sb("ah", [P, 2 * K16, 2, DH], F16)
        aT = sb("aT", [P, E, 2, SLOT])

        d_x = sem("d_x")
        d_w = sem("d_w")
        d_fw = sem("d_fw")
        d_ctx = [sem(f"d_ctx{k}") for k in range(4)]
        d_out = sem("d_out")
        c_zero = sem("c_zero")
        c_id = sem("c_id")
        c_dve = sem("c_dve")
        ln_bn = sem("ln_bn")
        ln_mv = sem("ln_mv")
        ln_var = sem("ln_var")
        ln_rstd = sem("ln_rstd")
        ln_x = sem("ln_x")
        c_bk = sem("c_bk")
        pe_bk = sem("pe_bk")
        bkq_out = sem("bkq_out")
        xbk = sem("xbk")
        cq_r = sem("cq_r")
        c_xbv = sem("c_xbv")
        fp_pe = sem("fp_pe")
        fp_act = sem("fp_act")
        fp_dve = sem("fp_dve")
        f_xh = sem("f_xh")
        f_xl = sem("f_xl")
        ln_sqrt = sem("ln_sqrt")
        su_pe = sem("su_pe")
        su_act = sem("su_act")
        su_dve = sem("su_dve")
        qkc = sem("qkc")
        nathi = sem("nathi")
        natlo = sem("natlo")
        natlo2 = sem("natlo2")
        tfull = sem("tfull")
        tev_d = sem("tev_d")
        tev_a = sem("tev_a")
        st_done = sem("st_done")
        tmx = sem("tmx")
        tmT = sem("tmT")
        mred = sem("mred")
        nsh = sem("nsh")
        dghi = sem("dghi")
        dgr = sem("dgr")
        shd = sem("shd")
        expd = sem("expd")
        plo = sem("plo")
        pvd = sem("pvd")
        dend = sem("dend")
        rdn = sem("rdn")
        aor = sem("aor")
        prj = sem("prj")
        x2d = sem("x2d")
        bsd = sem("bsd")
        mvd = sem("mvd")
        mvc = sem("mvc")
        x2c = sem("x2c")
        l2a = sem("l2a")
        l2b = sem("l2b")
        l2c = sem("l2c")
        f_xn = sem("f_xn")
        f_xnT = sem("f_xnT")
        f_xnTe = sem("f_xnTe")
        f_g = sem("f_g")
        f_ge = sem("f_ge")
        f_th = sem("f_th")
        f_pj = sem("f_pj")
        f_pje = sem("f_pje")
        f_z1 = sem("f_z1")
        f_z2 = sem("f_z2")
        f_z1e = sem("f_z1e")
        f_z2e = sem("f_z2e")
        f_s = sem("f_s")
        f_mx = sem("f_mx")
        f_sub = sem("f_sub")
        f_e = sem("f_e")
        f_rs = sem("f_rs")
        f_ri = sem("f_ri")
        f_top = sem("f_top")
        f_mo = sem("f_mo")
        f_sg = sem("f_sg")
        f_mix = sem("f_mix")
        f_tr = sem("f_tr")
        f_tre = sem("f_tre")
        f_d = sem("f_d")
        f_d2 = sem("f_d2")
        f_pjl = sem("f_pjl")
        f_ml = sem("f_ml")
        f_dm = sem("f_dm")
        f_et = sem("f_et")
        f_ete = sem("f_ete")
        f_vt = sem("f_vt")
        f_vte = sem("f_vte")
        f_vv = sem("f_vv")
        f_vve = sem("f_vve")
        f_pv = sem("f_pv")
        f_nrm = sem("f_nrm")
        f_ahi = sem("f_ahi")
        f_alo = sem("f_alo")
        f_a = sem("f_a")
        f_ae = sem("f_ae")
        f_o = sem("f_o")
        f_y = sem("f_y")
        t_ = [sem(f"top_step{n}") for n in range(10)]


        def after(eng, s, value):
            if not isinstance(value, int) or value > 0:
                eng.wait_ge(s, value)

        NW, NFW = 6, 7
        NG = 4
        GW = B * S // NG
        block = es.enter_context(nc.Block())

        @block.sync
        def _(sp):
            sp.wait_ge(c_zero, 1)
            for b in range(2):
                sp.dma_start(x_all[SLOT * b:SLOT * b + S, :].rearrange("t (p c) -> t p c", c=C), x_v[b]).then_inc(d_x, 16)
            for dst, src in ((wq_nat[:, :], wq), (wk_nat[:, :], wk), (wv_nat[:, :], wv),
                             (bq_col[:, :], bq.rearrange("(d o) -> d o", o=1)), (bk_col[:, :], bk.rearrange("(d o) -> d o", o=1)),
                             (bv_all[:, :], bv.rearrange("(o d) -> o d", o=1).broadcast_to((P, C)))):
                sp.dma_start(dst, src).then_inc(d_w, 16)

            def load(k, n):
                sp.dma_start(ctxf[k][:, 0:RPP * C], ctx[n, 0:RPP * P, :].rearrange("(p r) c -> p (r c)", r=RPP)).then_inc(d_ctx[k], 16)
                sp.dma_start(ctxf[k][0:REST, RPP * C:], ctx[n, RPP * P:L, :]).then_inc(d_ctx[k], 16)
                sp.dma_start(ctxf[k][REST:P, RPP * C:], ctx[n, L - DUP:L, :]).then_inc(d_ctx[k], 16)

            for k in range(4):
                load(k, k)
            for dst, src in (
                (fwq_nat[:, :, :], fwq.rearrange("(k h) d c -> (h d) k c", h=2)),
                (fwk_nat[:, :, :], fwk.rearrange("(k h) d c -> (h d) k c", h=2)),
                (fwv_nat[:, :, :], fwv.rearrange("(k e) d c -> (e d) k c", e=2)),
                (fws_nat[:, :], fws.rearrange("h e c -> (h e) c")),
                (fwd_nat[:, :], fwd.rearrange("h e c -> (h e) c")),
                (fwo_nat[:, :, 0, :], fwo.rearrange("e f d -> f e d")),
                (fwo_nat[:, :, 1, :], fwo.rearrange("e f d -> f e d")),
            ):
                sp.dma_start(dst, src).then_inc(d_fw, 16)

            def loads(i):
                for k in range(4):
                    n = 4 * i + k
                    after(sp, nathi, n - 3)
                    after(sp, natlo, n - 3)
                    after(sp, natlo2, n - 3)
                    sp_load(k, n)

            def sp_load(k, n):
                flat = ctx.rearrange("n l c -> (n l) c")
                sp.dma_start(ctxf[k][:, 0:RPP * C],
                             flat[bass.ds(n * L, RPP * P), :].rearrange("(p r) c -> p (r c)", r=RPP)).then_inc(d_ctx[k], 16)
                sp.dma_start(ctxf[k][0:REST, RPP * C:], flat[bass.ds(n * L + RPP * P, REST), :]).then_inc(d_ctx[k], 16)
                sp.dma_start(ctxf[k][REST:P, RPP * C:], flat[bass.ds(n * L + L - DUP, DUP), :]).then_inc(d_ctx[k], 16)

            with sp.Fori(1, NP // 2) as i:
                loads(i)
            with sp.Fori(0, NP) as i:
                after(sp, f_y, i + 1)
                for b in range(2):
                    sp.dma_start(out.rearrange("n t c -> (n t) c")[bass.ds(i * (2 * S) + b * S, S), :],
                                 y_all[SLOT * b:SLOT * b + S, bass.ds(i * C, C)]).then_inc(d_out, 16)
            sp.wait_ge(d_out, 32 * NP)

        @block.gpsimd
        def _(pool):
            pool.memset(x_all[:, :], 0.0).then_inc(c_zero, 1)
            pool.memset(ident[:, :], 0.0).then_inc(c_id, 1)
            pool.wait_ge(c_id, 1)
            pool.affine_select(out=ident[:, :], in_=ident[:, :], compare_op=ALU.not_equal, fill=1.0, base=0,
                               pattern=[[-1, P]], channel_multiplier=1).then_inc(c_id, 1)
            pool.memset(qT[:, :, :], 0.0).then_inc(c_zero, 1)
            pool.memset(tmax[:, :, :], 0.0).then_inc(c_zero, 1)
            pool.memset(p16[:, 0, :, :, :], 1.0).then_inc(c_zero, 1)
            pool.memset(p16[:, 1, :, :, :], 0.0).then_inc(c_zero, 1)
            pool.memset(aoT[:, :, :], 0.0).then_inc(c_zero, 1)
            pool.memset(rows_of[:, :, :], 0.0).then_inc(c_zero, 1)
            pool.memset(ones16[:, :], 1.0).then_inc(c_zero, 1)
            pool.wait_ge(c_zero, 8)
            for b in range(2):
                pool.memset(rows_of[SLOT * b:SLOT * b + SLOT, b, :], -1.0).then_inc(c_zero, 1)
            pool.wait_ge(c_zero, 10)
            for e in range(E):
                pool.memset(rank[:, :, e], float(E - e)).then_inc(c_zero, 1)
            pool.memset(e_sb[:, :, :, :], 0.0).then_inc(c_zero, 1)
            pool.memset(vT[:, :, :, :], 0.0).then_inc(c_zero, 1)
            pool.memset(aT[:, :, :, :], 0.0).then_inc(c_zero, 1)
            pool.memset(xnT[:, :], 0.0).then_inc(c_zero, 1)
            pool.memset(eT[:, :, :, :], 0.0).then_inc(c_zero, 1)

            def low_rows(n, k):
                after(pool, nathi, n + 1)
                pool.tensor_tensor(nat[k][:, 1, 7 * C:], ctxf[k][:, 7 * C:], nat[k][:, 0, 7 * C:], ALU.subtract).then_inc(natlo2, 1)

            def low_probs(n, b, pair):
                after(pool, expd, 2 * n + 2)
                after(pool, dend, pair)
                pool.tensor_tensor(p16[:, 1, :, b, 0:S], pf[b][:, :, :], p16[:, 0, :, b, 0:S], ALU.subtract).then_inc(plo, 1)

            def keep(pair):
                after(pool, x2d, pair + 1)
                pool.tensor_copy(x2_all[:, bass.ds(pair * C, C)], x2_cur[:, :]).then_inc(x2c, 1)

            def queries(pair, s):
                after(pool, st_done, 2 * pair - 2)
                pool.tensor_copy(qk_cur[s][:, :, :], qk_all[:, :, bass.ds(pair * (2 * S), 2 * S)]).then_inc(qkc, 1)

            def steps(i):
                for s in range(2):
                    pair = 2 * i + s
                    n = 2 * pair
                    first = isinstance(pair, int) and pair == 0
                    more = not (isinstance(pair, int) and pair == NP - 1)
                    if more:
                        low_rows(n + 2, (2 * s + 2) % 4)
                        low_rows(n + 3, (2 * s + 3) % 4)
                        queries(pair + 1, 1 - s)
                    low_probs(n, 0, pair)
                    low_probs(n + 1, 1, pair)
                    if not first:
                        keep(pair - 1)

            pool.wait_ge(bkq_out, 1)
            pool.wait_ge(ln_x, NG)
            pool.tensor_tensor(x2_all[:, :].rearrange("p (n c) -> p n c", c=C), y_all[:, :].rearrange("p (n c) -> p n c", c=C),
                               bkq[:, 0:C].unsqueeze(1).broadcast_to((P, NP, C)), ALU.mult).then_inc(xbk, 1)
            low_rows(0, 0)
            low_rows(1, 1)
            pool.wait_ge(su_dve, NG)
            queries(0, 0)
            steps(0)
            with pool.Fori(1, NP // 2 - 1) as i:
                steps(i)
            steps(NP // 2 - 1)
            keep(NP - 1)

            def masks(i):
                after(pool, f_mo, i + 1)
                after(pool, f_a, i)
                pool.tensor_tensor(dm[:, :, :, :], chosen[:, NQ * HG:, :].unsqueeze(2).broadcast_to((P, NQ * HG, HALF, E)),
                                   diag_e[:, :, :].unsqueeze(1).broadcast_to((P, NQ * HG, HALF, E)), ALU.mult).then_inc(f_dm, 1)

            def low_tokens(i):
                after(pool, f_xnTe, i + 1)
                after(pool, f_xh, i + 1)
                pool.tensor_tensor(xn16[:, 1, :], xnT[:, 0:2 * S], xn16[:, 0, :], ALU.subtract).then_inc(f_xl, 1)

            def weights(i):
                after(pool, f_tre, i + 1)
                after(pool, f_vt, i)
                n = 2 * NQ - DVE_K
                for part in range(2):
                    if part == 1:
                        after(pool, f_ml, i + 1)
                    last = pool.tensor_tensor(dv[:, part, DVE_K:, :, :],
                                              mixp[:, part, DVE_K:, :].unsqueeze(2).broadcast_to((P, n, HALF, H)),
                                              diag_h[:, :, :].unsqueeze(1).broadcast_to((P, n, HALF, H)), ALU.mult)
                last.then_inc(f_d2, 1)

            def low_experts(i):
                after(pool, f_pje, i + 1)
                after(pool, f_vt, i)
                pool.tensor_tensor(pj[:, 1, :, :], pjf[:, :, :], pj[:, 0, :, :], ALU.subtract).then_inc(f_pjl, 1)

            pool.wait_ge(c_dve, 11)
            pool.wait_ge(mvd, NP)
            def after_choice(i, nxt=True):
                low_experts(i)
                weights(i)
                if nxt:
                    low_tokens(i + 1)
                masks(i)

            low_tokens(0)
            after_choice(0)
            with pool.Fori(1, NP - 1) as i:
                after_choice(i)
            after_choice(NP - 1, nxt=False)

        @block.scalar
        def _(act):
            act.wait_ge(su_pe, 1)
            act.copy(wqT[:, :], ps[:, 0, 0:P])
            act.copy(wvT[:, :], ps[:, 0, P:2 * P]).then_inc(su_act, 1)
            for g in range(NG):
                act.wait_ge(ln_var, g + 1)
                act.sqrt(st_std[:, 4 * g:4 * g + 4], st_ve[:, 4 * g:4 * g + 4]).then_inc(ln_sqrt, 1)
            for g in range(NG):
                act.wait_ge(su_pe, 2 + g)
                act.copy(xn1T[:, GW * g:GW * (g + 1)].rearrange("p (n t) -> p n t", t=S),
                         ps[:, (5, 6, 7, 0)[g], :].rearrange("p (n t) -> p n t", t=SLOT)[:, :, 0:S]).then_inc(su_act, 1)
            act.wait_ge(c_zero, 2)
            for g in range(NG):
                act.wait_ge(su_pe, 2 + NG + g)
                act.activation(qT[:, 8 * g:8 * g + 8, 0:S], ps[:, 1 + g, 0:GW].rearrange("p (n t) -> p n t", t=S),
                               ACT.Identity, bias=bq_col[:, 0:1]).then_inc(su_act, 1)
            for g in range(NG):
                act.wait_ge(su_pe, 2 + 2 * NG + g)
                act.copy(qk_all[:, 0, GW * g:GW * (g + 1)], ps[:, (5, 6, 7, 0)[g], 0:GW]).then_inc(su_act, 1)

            def split_hi(n, k, turn):
                act.wait_ge(d_ctx[k], 48 * (turn + 1))
                after(act, pvd, n - 3)
                act.copy(nat[k][:, 0, :], ctxf[k][:, :]).then_inc(nathi, 1)

            def t_evac(n, b):
                after(act, tfull, 3 * n + 2)
                after(act, st_done, n - 1)
                act.copy(ctxT[b][:, 8 * P:16 * P], ps[:, (3 * b + 1) % 2, :].bitcast(F16)).then_inc(tev_a, 1)

            def exps(n, b, pair):
                after(act, shd, n + 1)
                after(act, dend, pair)
                act.activation(p16[:, 0, :, b, 0:S].rearrange("p (a t) q -> p a t q", a=2),
                               ps[:, 2 + 2 * b:4 + 2 * b, 0:6 * S].rearrange("p a (t q) -> p a t q", t=6), ACT.Exp).then_inc(expd, 1)
                act.activation(pf[b][:, :, :].rearrange("p (a t) q -> p a (t q)", a=2),
                               ps[:, 2 + 2 * b:4 + 2 * b, 0:6 * S], ACT.Exp).then_inc(expd, 1)

            def steps(i):
                for s in range(2):
                    pair = 2 * i + s
                    n = 2 * pair
                    more = not (isinstance(pair, int) and pair == NP - 1)
                    if more:
                        split_hi(n + 2, (2 * s + 2) % 4, i + s)
                        split_hi(n + 3, (2 * s + 3) % 4, i + s)
                        t_evac(n + 2, 0)
                    exps(n, 0, pair)
                    exps(n + 1, 1, pair)
                    if more:
                        t_evac(n + 3, 1)

            split_hi(0, 0, 0)
            split_hi(1, 1, 0)
            t_evac(0, 0)
            t_evac(1, 1)
            act.wait_ge(c_zero, 5)
            steps(0)
            with act.Fori(1, NP // 2 - 1) as i:
                steps(i)
            steps(NP // 2 - 1)

            act.wait_ge(fp_pe, 1)
            act.copy(fwvT[:, :, :], ps[:, 0, :].rearrange("p (e d) -> p e d", e=E)).then_inc(fp_act, 1)
            act.wait_ge(fp_pe, 2)
            for g in range(2):
                last = act.copy(wg[:, :, g, :, :].rearrange("p a b e -> p b a e"),
                                ps[:, 1, P * g:P * g + P].rearrange("p (b a e) -> p b a e", b=HG, a=4))
            last.then_inc(fp_act, 1)
            act.wait_ge(fp_pe, 3)
            act.copy(wo2[:, :, :], ps[:, 2:4, :].rearrange("p a (e f) -> p (a e) f", f=C)).then_inc(fp_act, 1)
            mT_v = mT[:, 0, :, :].rearrange("p (a k h) c -> p h a k c", a=2, h=2)
            for h2 in range(2):
                act.wait_ge(fp_pe, 4 + h2)
                for a in range(2):
                    last = act.copy(mT_v[:, h2, a, :, :], ps[:, 4 * h2 + a, :].rearrange("p (k c) -> p k c", c=C))
                last.then_inc(fp_act, 1)
            act.wait_ge(l2a, 1)
            act.sqrt(st_std[:, :], st_ve[:, :]).then_inc(l2b, 1)

            def xnT_evac(i):
                after(act, f_xnT, i + 1)
                after(act, f_s, i)
                act.copy(xnT[:, 0:2 * S].rearrange("p (b t) -> p b t", b=2),
                         ps[:, 2, 0:P].rearrange("p (b t) -> p b t", b=2)[:, :, 0:S]).then_inc(f_xnTe, 1)
                act.copy(xn16[:, 0, :].rearrange("p (b t) -> p b t", b=2),
                         ps[:, 2, 0:P].rearrange("p (b t) -> p b t", b=2)[:, :, 0:S]).then_inc(f_xh, 1)

            def gates_out(i):
                after(act, f_g, i + 1)
                after(act, f_top, i)
                act.copy(g_sb[:, :, :].rearrange("p (g q n) e -> p q g (n e)", g=2, q=NQ),
                         ps[:, 2, 0:2 * P].rearrange("p (q g m) -> p q g m", q=NQ, g=2)).then_inc(f_ge, 1)
                act.wait_ge(f_ge, i + 1)
                after(act, f_sg, i)
                act.activation(th[:, :, :], g_sb[:, 0:16, :], ACT.Tanh, scale=0.5).then_inc(f_th, 1)

            def iteration(i, front=True, back=True, nxt=True):
                if back:
                    after(act, f_vt, i)
                    after(act, f_vv, i - 1)
                    act.mul(vT[:, :, :, 0:S].rearrange("p h b t -> p b t h"),
                            ps[:, 6:8, 0:8 * S].rearrange("p b (t h) -> p b t h", h=8), 1.0 / (MIX_UP * PJ_UP)).then_inc(f_vte, 1)
                if front:
                    after(act, f_pj, i + 1)
                    after(act, f_vt, i)
                    after(act, f_pjl, i)
                    act.mul(pjf[:, :, :], ps[:, 3, :].rearrange("p (q d) -> p q d", d=DH), PJ_UP)
                    act.mul(pj[:, 0, :, :], ps[:, 3, :].rearrange("p (q d) -> p q d", d=DH), PJ_UP).then_inc(f_pje, 1)
                    after(act, f_z1, i + 1)
                    after(act, f_s, i)
                    act.mul(z[:, 0:8, :].rearrange("p (a k) n -> p a (k n)", a=2), ps[:, 0:2, 0:8 * S], SCALE).then_inc(f_z1e, 1)
                    after(act, f_tr, i + 1)
                    after(act, f_d, i)
                    after(act, f_d2, i)
                    act.mul(mixp[:, 0, :, :], ps[:, 3, 0:P].rearrange("p (q h) -> p q h", h=H), MIX_UP)
                    act.mul(mixf[:, :, :], ps[:, 3, 0:P].rearrange("p (q h) -> p q h", h=H), MIX_UP).then_inc(f_tre, 1)
                if back:
                    after(act, f_vv, i)
                    after(act, f_pv, 2 * i - 2)
                    act.copy(v_sb[:, :, :].rearrange("p (a h) d -> p a (h d)", a=2), ps[:, 4:6, :]).then_inc(f_vve, 1)
                if front:
                    after(act, f_z2, i + 1)
                    after(act, f_s, i)
                    act.mul(z[:, 8:16, :].rearrange("p (a k) n -> p a (k n)", a=2), ps[:, 2:4, 0:8 * S], SCALE).then_inc(f_z2e, 1)
                if nxt:
                    xnT_evac(i + 1)
                if back:
                    after(act, f_a, i)
                    after(act, f_o, i - 1)
                    act.copy(aT[:, :, :, 0:S].rearrange("p e b t -> p b t e"),
                             ps[:, 4:6, 0:8 * S].rearrange("p b (t e) -> p b t e", e=E)).then_inc(f_ae, 1)
                if front:
                    after(act, f_sub, i + 1)
                    after(act, f_et, i)
                    after(act, f_rs, i)
                    act.activation(e_sb[:, :, :, 0:S].rearrange("p k b j -> p b k j"),
                                   ssub[:, :, :].rearrange("p (b k) j -> p b k j", b=2), ACT.Exp).then_inc(f_e, 1)
                if nxt:
                    gates_out(i + 1)
                if front:
                    after(act, f_et, i + 1)
                    after(act, f_pv, 2 * i)
                    for b in range(2):
                        r = slice(SLOT * b, SLOT * b + SLOT)
                        act.copy(eT[r, b, :, :].rearrange("p (a k) n -> p a (k n)", a=2), ps[r, 0:2, :]).then_inc(f_ete, 1)

            act.wait_ge(c_zero, 23)
            xnT_evac(0)
            gates_out(0)
            iteration(0, back=False)
            iteration(1)
            with act.Fori(2, NP - 1) as i:
                iteration(i)
            iteration(NP - 1, nxt=False)
            iteration(NP, front=False, nxt=False)

        @block.vector
        def _(dve):
            v3 = lambda t: t[:, :].rearrange("p (n c) -> p n c", c=C)
            dve.wait_ge(c_id, 2)
            dve.tensor_copy(ident16[:, :], ident[:, :]).then_inc(c_dve, 1)
            for b in range(2):
                dve.tensor_copy(diag_q[SLOT * b:SLOT * b + SLOT, :], ident[SLOT * b:SLOT * b + SLOT, SLOT * b:SLOT * b + S]).then_inc(c_dve, 1)
            dve.wait_ge(d_w, 16 * NW)
            dve.tensor_copy(bk_rep[:, :], bk_col[:, 0:1].broadcast_to((P, C))).then_inc(c_bk, 1)
            dve.wait_ge(d_x, 32)

            def ln_stats(g):
                for n in range(4 * g, 4 * g + 4):
                    last = dve.bn_stats(bst_all[:, n, :], x_all[:, C * n:C * n + C])
                last.then_inc(ln_bn, 1)
                dve.wait_ge(ln_bn, g + 1)
                for n in range(4 * g, 4 * g + 4):
                    last = dve.bn_aggr(mv_all[:, 2 * n:2 * n + 2], bst_all[:, n, :])
                last.then_inc(ln_mv, 1)
                dve.wait_ge(ln_mv, g + 1)
                dve.tensor_scalar(st_ve[:, 4 * g:4 * g + 4], mv_all[:, :].rearrange("p (n k) -> p n k", k=2)[:, 4 * g:4 * g + 4, 1],
                                  EPS, None, ALU.add).then_inc(ln_var, 1)

            def ln_apply(g):
                dve.wait_ge(ln_sqrt, g + 1)
                dve.reciprocal(st_rstd[:, 4 * g:4 * g + 4], st_std[:, 4 * g:4 * g + 4]).then_inc(ln_rstd, 1)
                dve.wait_ge(ln_rstd, g + 1)
                for n in range(4 * g, 4 * g + 4):
                    last = dve.tensor_scalar(y_all[:, C * n:C * n + C], x_all[:, C * n:C * n + C], mv_all[:, 2 * n:2 * n + 1],
                                             st_rstd[:, n:n + 1], ALU.subtract, ALU.mult)
                last.then_inc(ln_x, 1)

            dve.wait_ge(pe_bk, 1)
            dve.tensor_copy(bkq[:, :], ps[:, 1, 0:C + 1]).then_inc(bkq_out, 1)
            ln_stats(0)
            for g in range(NG):
                if g + 1 < NG:
                    ln_stats(g + 1)
                ln_apply(g)
            dve.wait_ge(ln_x, NG)
            dve.tensor_tensor(v3(x_all), v3(x_all), bv_all[:, :].unsqueeze(1).broadcast_to((P, NP, C)), ALU.add).then_inc(c_xbv, 1)
            for q in range(4):
                r = slice(32 * q, 32 * q + 32)
                cut = ident[r, 32 * q:32 * q + HALF].unsqueeze(2)
                dve.tensor_copy(diag_h[r, :, :], cut.broadcast_to((32, HALF, H))).then_inc(c_dve, 1)
                dve.tensor_copy(diag_e[r, :, :], cut.broadcast_to((32, HALF, E))).then_inc(c_dve, 1)
            for g in range(NG):
                dve.wait_ge(su_act, 2 + 2 * NG + g)
                dve.tensor_tensor(qk_all[:, 1, GW * g:GW * (g + 1)], ps[:, (5, 6, 7, 0)[g], 0:GW],
                                  qk_all[:, 0, GW * g:GW * (g + 1)], ALU.subtract).then_inc(su_dve, 1)

            def split_lo(n, k):
                after(dve, nathi, n + 1)
                dve.tensor_tensor(nat[k][:, 1, 0:7 * C], ctxf[k][:, 0:7 * C], nat[k][:, 0, 0:7 * C],
                                  ALU.subtract).then_inc(natlo, 1)

            def t_evac(n, b, c):
                after(dve, tfull, 3 * n + c + 1)
                after(dve, st_done, n - 1)
                dve.tensor_copy(ctxT[b][:, 8 * P * c:8 * P * (c + 1)], ps[:, (3 * b + c) % 2, :].bitcast(F16)).then_inc(tev_d, 1)

            def tile_max(n, pair, b):
                after(dve, st_done, n + 1)
                after(dve, tmT, pair)
                dve.tensor_reduce(tmax[:, b, 0:S], ps[:, 2 + 2 * b:4 + 2 * b, 0:6 * S].rearrange("p a (t q) -> p q a t", t=6),
                                  AX.XY, ALU.max).then_inc(tmx, 1)

            def shifts(pair):
                after(dve, tmT, pair + 1)
                dve.tensor_reduce(m_q[:, :], ps[:, 7, 0:P], AX.X, ALU.max).then_inc(mred, 1)
                dve.wait_ge(mred, pair + 1)
                dve.scalar_tensor_tensor(nshift[:, :], m_q[:, :], cq[:, bass.ds(pair, 1)], cq[:, bass.ds(pair, 1)],
                                         op0=ALU.add, op1=ALU.subtract).then_inc(nsh, 1)
                dve.wait_ge(nsh, pair + 1)
                after(dve, shd, 2 * pair)
                dve.tensor_scalar(dg[:, 0, :], diag_q[:, :], nshift[:, 0:1], None, ALU.mult).then_inc(dghi, 1)
                dve.wait_ge(dghi, pair + 1)
                dve.scalar_tensor_tensor(dg[:, 1, :], diag_q[:, :], nshift[:, 0:1], dg[:, 0, :],
                                         op0=ALU.mult, op1=ALU.subtract).then_inc(dgr, 1)

            def sums_out(pair):
                after(dve, pvd, 2 * pair + 2)
                after(dve, dend, pair + 1)
                after(dve, prj, pair)
                dve.tensor_copy(aoT[:, :, 0:S], ps[:, 6, 0:P].rearrange("p (b q) -> p b q", b=2)[:, :, 0:S]).then_inc(aor, 1)

            def den_out(pair):
                dve.reciprocal(rden[:, :], ps[:, 6, P:P + 1]).then_inc(rdn, 1)

            def result(pair):
                after(dve, rdn, pair + 1)
                after(dve, x2c, pair)
                after(dve, prj, pair + 1)
                dve.scalar_tensor_tensor(x2_cur[:, :], ps[:, 6, 2 * P:3 * P], rden[:, 0:1],
                                         x_all[:, bass.ds(pair * C, C)], op0=ALU.mult, op1=ALU.add).then_inc(x2d, 1)

            def moments(pair):
                dve.wait_ge(x2d, pair + 1)
                dve.bn_stats(bst[:, :], x2_cur[:, :]).then_inc(bsd, 1)
                dve.wait_ge(c_zero, 6)
                dve.wait_ge(bsd, pair + 1)
                dve.bn_aggr(mv_cur[:, :], bst[:, :]).then_inc(mvc, 1)
                dve.wait_ge(mvc, pair + 1)
                dve.tensor_copy(mv_all[:, bass.ds(pair * 2, 2)], mv_cur[:, :]).then_inc(mvd, 1)

            def steps(i):
                for s in range(2):
                    pair = 2 * i + s
                    n = 2 * pair
                    first = isinstance(pair, int) and pair == 0
                    more = not (isinstance(pair, int) and pair == NP - 1)
                    tile_max(n, pair, 0)
                    tile_max(n + 1, pair, 1)
                    shifts(pair)
                    if more:
                        split_lo(n + 2, (2 * s + 2) % 4)
                    if not first:
                        sums_out(pair - 1)
                    if more:
                        t_evac(n + 2, 0, 0)
                    if not first:
                        den_out(pair - 1)
                    if more:
                        split_lo(n + 3, (2 * s + 3) % 4)
                        t_evac(n + 2, 0, 2)
                        t_evac(n + 3, 1, 0)
                    if not first:
                        result(pair - 1)
                        moments(pair - 1)
                    if more:
                        t_evac(n + 3, 1, 2)

            for b in range(2):
                split_lo(b, b)
            for b in range(2):
                t_evac(b, b, 0)
                t_evac(b, b, 2)
            dve.wait_ge(xbk, 1)
            dve.tensor_reduce(cq_x[:, :], v3(x2_all), AX.X, ALU.add).then_inc(cq_r, 1)
            dve.wait_ge(cq_r, 1)
            dve.tensor_scalar(cq[:, :], cq_x[:, :], bkq[:, C:C + 1], None, ALU.add).then_inc(su_dve, 1)
            dve.wait_ge(c_zero, 6)
            dve.wait_ge(c_xbv, 1)
            dve.wait_ge(su_dve, NG + 1)
            steps(0)
            with dve.Fori(1, NP // 2 - 1) as i:
                steps(i)
            steps(NP // 2 - 1)
            sums_out(NP - 1)
            den_out(NP - 1)
            result(NP - 1)
            moments(NP - 1)

            mT_v = mT[:, :, :, :].rearrange("p s (a k h) c -> p s h a k c", a=2, h=2)
            for h2 in range(2):
                dve.wait_ge(fp_act, 4 + h2)
                for a in range(2):
                    last = dve.tensor_tensor(mT_v[:, 1, h2, a, :, :], ps[:, 4 * h2 + a, :].rearrange("p (k c) -> p k c", c=C),
                                             mT_v[:, 0, h2, a, :, :], ALU.subtract)
                last.then_inc(fp_dve, 1)
            dve.wait_ge(mvd, NP)
            dve.tensor_scalar(st_ve[:, :], mv_all[:, :].rearrange("p (n k) -> p n k", k=2)[:, :, 1], EPS, None, ALU.add).then_inc(l2a, 1)
            dve.wait_ge(l2b, 1)
            dve.reciprocal(st_rstd[:, :], st_std[:, :]).then_inc(l2c, 1)
            dve.wait_ge(l2c, 1)

            def normalise(i):
                after(dve, f_xnT, i)
                dve.tensor_scalar(xn[:, :], x2_all[:, bass.ds(i * C, C)], mv_all[:, bass.ds(i * 2, 1)],
                                  st_rstd[:, bass.ds(i, 1)], ALU.subtract, ALU.mult).then_inc(f_xn, 1)

            per8 = lambda t: t[:, :].unsqueeze(2).broadcast_to((P, 32, E))

            def top_two(i):
                after(dve, f_ge, i + 1)
                dve.tensor_reduce(m1[:, :], g_sb[:, :, :], AX.X, ALU.max).then_inc(t_[0], 1)
                dve.wait_ge(t_[0], i + 1)
                dve.tensor_tensor(eq1[:, :, :], g_sb[:, :, :], per8(m1), ALU.is_equal).then_inc(t_[1], 1)
                dve.wait_ge(t_[1], i + 1)
                dve.tensor_tensor(r1[:, :, :], eq1[:, :, :], rank[:, :, :], ALU.mult).then_inc(t_[2], 1)
                dve.wait_ge(t_[2], i + 1)
                dve.tensor_reduce(s1[:, :], r1[:, :, :], AX.X, ALU.max).then_inc(t_[3], 1)
                dve.wait_ge(t_[3], i + 1)
                dve.tensor_tensor(oh1[:, :, :], r1[:, :, :], per8(s1), ALU.is_equal).then_inc(t_[4], 1)
                dve.wait_ge(t_[4], i + 1)
                dve.scalar_tensor_tensor(g2[:, :, :], oh1[:, :, :], -3.0e38, g_sb[:, :, :], op0=ALU.mult, op1=ALU.add).then_inc(f_top, 1)

            def second(i):
                dve.wait_ge(f_top, i + 1)
                dve.tensor_reduce(m2[:, :], g2[:, :, :], AX.X, ALU.max).then_inc(t_[5], 1)
                dve.wait_ge(t_[5], i + 1)
                dve.tensor_tensor(eq2[:, :, :], g2[:, :, :], per8(m2), ALU.is_equal).then_inc(t_[6], 1)
                dve.wait_ge(t_[6], i + 1)
                dve.tensor_tensor(r2[:, :, :], eq2[:, :, :], rank[:, :, :], ALU.mult).then_inc(t_[7], 1)
                dve.wait_ge(t_[7], i + 1)
                dve.tensor_reduce(s2[:, :], r2[:, :, :], AX.X, ALU.max).then_inc(t_[8], 1)
                dve.wait_ge(t_[8], i + 1)
                dve.tensor_tensor(oh2[:, :, :], r2[:, :, :], per8(s2), ALU.is_equal).then_inc(t_[9], 1)
                dve.wait_ge(t_[9], i + 1)
                after(dve, f_dm, i)
                dve.tensor_tensor(chosen[:, :, :], oh1[:, :, :], oh2[:, :, :], ALU.add).then_inc(f_mo, 1)

            def mixing(i):
                after(dve, f_th, i + 1)
                dve.tensor_scalar(sg[:, :, :], th[:, :, :], 0.5, 0.5, ALU.mult, ALU.add).then_inc(f_sg, 1)
                dve.wait_ge(f_sg, i + 1)
                dve.wait_ge(f_mo, i + 1)
                after(dve, f_tr, i)
                dve.tensor_tensor(mix[:, :, :, :].rearrange("p q n e -> p (q n) e"), sg[:, :, :], chosen[:, 0:NQ * HG, :],
                                  ALU.mult).then_inc(f_mix, 1)

            def iteration(i, front=True, back=True, nxt=True):
                if front:
                    mixing(i)
                if nxt:
                    normalise(i + 1)
                if back:
                    after(dve, f_e, i)
                    dve.tensor_reduce(rs[:, :], e_sb[:, :, :, :].rearrange("p k b j -> p (k b) j"), AX.X, ALU.add).then_inc(f_rs, 1)
                    dve.wait_ge(f_rs, i)
                    dve.reciprocal(rinv[:, :], rs[:, :]).then_inc(f_ri, 1)
                if front:
                    after(dve, f_tre, i + 1)
                    after(dve, f_vt, i)
                    dve.tensor_tensor(mixp[:, 1, :, :], mixf[:, :, :], mixp[:, 0, :, :], ALU.subtract).then_inc(f_ml, 1)
                    dve.wait_ge(f_ml, i + 1)
                    for part in range(2):
                        last = dve.tensor_tensor(dv[:, part, 0:DVE_K, :, :],
                                                 mixp[:, part, 0:DVE_K, :].unsqueeze(2).broadcast_to((P, DVE_K, HALF, H)),
                                                 diag_h[:, :, :].unsqueeze(1).broadcast_to((P, DVE_K, HALF, H)), ALU.mult)
                    last.then_inc(f_d, 1)
                if back:
                    after(dve, f_ri, i)
                    after(dve, f_a, i - 1)
                    for b in range(2):
                        k = slice(K16 * b, K16 * b + K16)
                        after(dve, f_pv, 2 * i - 1 + b)
                        dve.tensor_tensor(attnf[:, k, :], ps[:, 6 + b, :].rearrange("p (k d) -> p k d", d=DH),
                                          rinv[:, :].rearrange("p (k b) -> p b k", b=2)[:, b, :].unsqueeze(2).broadcast_to((P, K16, DH)),
                                          ALU.mult).then_inc(f_nrm, 1)
                        dve.wait_ge(f_nrm, 2 * i - 1 + b)
                        dve.tensor_copy(ah[:, k, 0, :], attnf[:, k, :]).then_inc(f_ahi, 1)
                        dve.wait_ge(f_ahi, 2 * i - 1 + b)
                        dve.tensor_tensor(ah[:, k, 1, :], attnf[:, k, :], ah[:, k, 0, :], ALU.subtract).then_inc(f_alo, 1)
                if front:
                    after(dve, f_s, i + 1)
                    dve.tensor_reduce(smx[:, :], ps[:, 0:2, 0:8 * S].rearrange("p b (k j) -> p b k j", j=S), AX.X, ALU.max).then_inc(f_mx, 1)
                    dve.wait_ge(f_mx, i + 1)
                    after(dve, f_e, i)
                    dve.tensor_tensor(ssub[:, :, :].rearrange("p (b k) j -> p b k j", b=2),
                                      ps[:, 0:2, 0:8 * S].rearrange("p b (k j) -> p b k j", j=S),
                                      smx[:, :].rearrange("p (b k) -> p b k", b=2).unsqueeze(3).broadcast_to((P, 2, K16, S)),
                                      ALU.subtract).then_inc(f_sub, 1)
                if nxt:
                    top_two(i + 1)
                if back:
                    after(dve, f_o, i)
                    dve.tensor_tensor(y_all[:, bass.ds((i - 1) * C, C)], ps[:, 3, 0:C], x2_all[:, bass.ds((i - 1) * C, C)],
                                      ALU.add).then_inc(f_y, 1)
                if nxt:
                    second(i + 1)

            dve.wait_ge(c_zero, 23)
            dve.wait_ge(x2c, NP)
            normalise(0)
            top_two(0)
            second(0)
            iteration(0, back=False)
            iteration(1)
            with dve.Fori(2, NP - 1) as i:
                iteration(i)
            iteration(NP - 1, nxt=False)
            iteration(NP, front=False, nxt=False)

        @block.tensor
        def _(pe):
            pe.wait_ge(c_id, 2)
            pe.wait_ge(d_w, 16 * NW)
            pe.transpose(ps[:, 0, 0:P], wq_nat[:, :], ident[:, :])
            pe.transpose(ps[:, 0, P:2 * P], wv_nat[:, :], ident[:, :]).then_inc(su_pe, 1)
            pe.wait_ge(c_bk, 1)
            pe.matmul(ps[:, 1, 0:C], bk_rep[:, :], wq_nat[:, :], start=True, stop=True)
            pe.matmul(ps[:, 1, C:C + 1], bk_rep[:, :], bq_col[:, :], start=True, stop=True).then_inc(pe_bk, 1)
            for g in range(NG):
                pe.wait_ge(ln_x, g + 1)
                if g == NG - 1:
                    pe.wait_ge(su_act, 1)
                for k in range(4):
                    n = 4 * g + k
                    last = pe.transpose(ps[:, (5, 6, 7, 0)[g], P * k:P * k + P], y_all[:, C * n:C * n + C], ident[:, :])
                last.then_inc(su_pe, 1)
            pe.wait_ge(bkq_out, 1)
            for g in range(NG):
                pe.wait_ge(su_act, 2 + g)
                pe.matmul(ps[:, 1 + g, 0:GW], wqT[:, :], xn1T[:, GW * g:GW * (g + 1)], start=True, stop=True).then_inc(su_pe, 1)
            for g in range(NG):
                pe.wait_ge(su_act, 2 + NG + g)
                pe.matmul(ps[:, (5, 6, 7, 0)[g], 0:GW], wk_nat[:, :], qT[:, 8 * g:8 * g + 8, 0:S], start=True, stop=True).then_inc(su_pe, 1)
            pe.wait_ge(c_dve, 3)
            pe.wait_ge(su_dve, NG)
            pe.wait_ge(c_zero, 10)

            def turn(n, b, k, chunks=(0, 1, 2)):
                after(pe, nathi, n + 1)
                for c in chunks:
                    if c == 1:
                        after(pe, natlo, n + 1)
                    if c == 2:
                        after(pe, natlo2, n + 1)
                    if c == 0:
                        after(pe, tev_a, n)
                    elif c == 1:
                        after(pe, tev_d, 2 * n)
                    else:
                        after(pe, tev_d, 2 * n + 1)
                    for j in range(8 * c, 8 * c + 8):
                        last = pe.transpose(ps[:, (3 * b + c) % 2, :].bitcast(F16)[:, P * (j % 8):P * (j % 8) + P],
                                            nat[k][:, j // TK, C * (j % TK):C * (j % TK) + C], ident16[:, :])
                    last.then_inc(tfull, 1)

            def scores(n, pair, s, b):
                after(pe, tev_d, 2 * n + 2)
                after(pe, tev_a, n + 1)
                after(pe, qkc, pair + 1)
                after(pe, expd, 2 * n - 2)
                for t in range(TK):
                    o = ps[:, 2 + 2 * b + t // 6, S * (t % 6):S * (t % 6) + S]
                    hi = ctxT[b][:, P * t:P * t + P]
                    lo = ctxT[b][:, P * (TK + t):P * (TK + t) + P]
                    qh, ql = qk_cur[s][:, 0, S * b:S * b + S], qk_cur[s][:, 1, S * b:S * b + S]
                    pe.matmul(o, hi, qh, start=(t % 6 == 0), stop=False, skip_group_check=True)
                    pe.matmul(o, hi, ql, start=False, stop=False, skip_group_check=True)
                    last = pe.matmul(o, lo, qh, start=False, stop=False, skip_group_check=True)
                last.then_inc(st_done, 1)

            def max_turn(pair):
                after(pe, tmx, 2 * pair + 2)
                after(pe, mred, pair)
                pe.transpose(ps[:, 7, 0:P], tmax[:, :, :].rearrange("p b q -> p (b q)"), ident[:, :]).then_inc(tmT, 1)

            def shift(n, pair, b):
                after(pe, dgr, pair + 1)
                for a in range(2):
                    o = ps[:, 2 + 2 * b + a, 0:6 * S].rearrange("p (t q) -> p t q", t=6)
                    for part in range(2):
                        last = pe.matmul(o, rows_of[:, b, :],
                                         dg[:, part, :].unsqueeze(1).broadcast_to((P, 6, S)),
                                         start=False, stop=(part == 1), skip_group_check=True)
                last.then_inc(shd, 1)

            def values(n, pair, b, k):
                after(pe, plo, n + 1)
                if b == 0:
                    after(pe, x2d, pair)
                o = ps[:, 6, SLOT * b:SLOT * b + S]
                for t in range(TK):
                    r = slice(0, P if t < TK - 1 else REST)
                    hi, lo = nat[k][r, 0, C * t:C * t + C], nat[k][r, 1, C * t:C * t + C]
                    ph, pl = p16[r, 0, t, b, 0:S], p16[r, 1, t, b, 0:S]
                    pe.matmul(o, hi, ph, start=(t == 0), stop=False)
                    pe.matmul(o, hi, pl, start=False, stop=False)
                    last = pe.matmul(o, lo, ph, start=False, stop=(t == TK - 1))
                last.then_inc(pvd, 1)

            def denominator(pair):
                for part in range(2):
                    for t in range(TK):
                        r = slice(0, P if t < TK - 1 else REST)
                        last = pe.matmul(ps[:, 6, P:P + 1], p16[r, part, t, :, :].rearrange("p b q -> p (b q)"), ones16[r, :],
                                         start=(part == 0 and t == 0), stop=(part == 1 and t == TK - 1))
                last.then_inc(dend, 1)

            def project(pair):
                after(pe, aor, pair + 1)
                after(pe, rdn, pair + 1)
                pe.matmul(ps[:, 6, 2 * P:3 * P], aoT[:, :, :].rearrange("p b q -> p (b q)"), wvT[:, :], start=True, stop=True).then_inc(prj, 1)

            def steps(i):
                for s in range(2):
                    pair = 2 * i + s
                    n = 2 * pair
                    first = isinstance(pair, int) and pair == 0
                    more = not (isinstance(pair, int) and pair == NP - 1)
                    k0, k1 = (2 * s + 2) % 4, (2 * s + 3) % 4
                    scores(n, pair, s, 0)
                    scores(n + 1, pair, s, 1)
                    if not first:
                        values(n - 2, pair - 1, 0, k0)
                    max_turn(pair)
                    if not first:
                        values(n - 1, pair - 1, 1, k1)
                        denominator(pair - 1)
                    if more:
                        turn(n + 2, 0, k0, (0,))
                    shift(n, pair, 0)
                    if more:
                        turn(n + 2, 0, k0, (1,))
                    shift(n + 1, pair, 1)
                    if not first:
                        project(pair - 1)
                    if more:
                        turn(n + 2, 0, k0, (2,))
                        turn(n + 3, 1, k1, (0,))
                        turn(n + 3, 1, k1, (1,))
                        turn(n + 3, 1, k1, (2,))

            for b in range(2):
                turn(b, b, b)
            steps(0)
            with pe.Fori(1, NP // 2 - 1) as i:
                steps(i)
            steps(NP // 2 - 1)
            pe.wait_ge(d_fw, 16 * NFW)
            pe.wait_ge(tev_d, 4 * NP)
            pe.wait_ge(tev_a, 2 * NP)
            for k in range(E // 2):
                last = pe.transpose(ps[:, 0, P * k:P * k + P], fwv_nat[:, k, :], ident[:, :])
            last.then_inc(fp_pe, 1)
            pe.transpose(ps[:, 1, 0:P], fws_nat[:, :], ident[:, :])
            pe.transpose(ps[:, 1, P:2 * P], fwd_nat[:, :], ident[:, :]).then_inc(fp_pe, 1)
            pe.wait_ge(expd, 4 * NP - 2)
            for e in range(E):
                last = pe.transpose(ps[:, 2 + e // 4, P * (e % 4):P * (e % 4) + P], fwo_nat[:, e, :, :].rearrange("p a d -> p (a d)"), ident[:, :])
            last.then_inc(fp_pe, 1)

            def head_products(h2):
                for a in range(2):
                    for k in range(4):
                        last = pe.matmul(ps[:, 4 * h2 + a, P * k:P * k + P], fwk_nat[DH * h2:DH * h2 + DH, 4 * a + k, :],
                                         fwq_nat[DH * h2:DH * h2 + DH, 4 * a + k, :], start=True, stop=True)
                last.then_inc(fp_pe, 1)

            values(2 * NP - 2, NP - 1, 0, 2)
            pe.wait_ge(fp_act, 2)
            head_products(0)
            values(2 * NP - 1, NP - 1, 1, 3)
            denominator(NP - 1)
            project(NP - 1)
            pe.wait_ge(expd, 4 * NP)
            head_products(1)

            def xn_turn(i):
                after(pe, f_xn, i + 1)
                after(pe, f_z2e, i)
                pe.transpose(ps[:, 2, 0:P], xn[:, :], ident[:, :]).then_inc(f_xnT, 1)

            def z_heads(h0, first_bank):
                for h in range(h0, h0 + 8):
                    k = h - h0
                    o = ps[:, first_bank + k // 4, 2 * S * (k % 4):2 * S * (k % 4) + 2 * S]
                    pe.matmul(o, mT[:, 0, h, :], xn16[:, 0, :], start=True, stop=False)
                    pe.matmul(o, mT[:, 0, h, :], xn16[:, 1, :], start=False, stop=False)
                    last = pe.matmul(o, mT[:, 1, h, :], xn16[:, 0, :], start=False, stop=True)
                return last

            def gates(i):
                after(pe, f_xnTe, i + 1)
                after(pe, f_xh, i + 1)
                for q in range(NQ):
                    for h4 in range(4):
                        last = pe.matmul(ps[32 * h4:32 * h4 + 32, 2, 64 * q:64 * q + 64], xnT[:, HALF * q:HALF * q + 32],
                                         wg[:, h4, :, :, :].rearrange("p g n e -> p (g n e)"), start=True, stop=True)
                last.then_inc(f_g, 1)

            def iteration(i, front=True, back=True, nxt=True):
                if back:
                    after(pe, f_d, i)
                    after(pe, f_d2, i)
                    after(pe, f_pjl, i)
                    after(pe, f_pje, i)
                    after(pe, f_nrm, 2 * i - 2)
                    for q in range(NQ):
                        for k in (2 * q, 2 * q + 1):
                            for a, b in ((0, 0), (0, 1), (1, 0)):
                                for par in range(2):
                                    o = ps[DH * par:DH * par + DH, 6 + q // 2, 224 * (q % 2):224 * (q % 2) + 224].rearrange("p (t h) -> p t h", h=8)
                                    last = pe.matmul(o, pj[:, a, k, :], dv[:, b, k, :, 8 * par:8 * par + 8],
                                                     start=(k % 2 == 0 and a + b == 0), stop=(k % 2 == 1 and a == 1))
                    last.then_inc(f_vt, 1)
                if front:
                    after(pe, f_y, i - 1)
                    for q in range(NQ):
                        for e4 in range(4):
                            last = pe.matmul(ps[32 * e4:32 * e4 + 32, 3, P * q:P * q + P].rearrange("p (a d) -> p a d", a=2),
                                             xnT[:, HALF * q:HALF * q + 32],
                                             fwvT[:, e4::4, :], start=True, stop=True)
                    last.then_inc(f_pj, 1)
                    after(pe, f_ete, 2 * i)
                    after(pe, f_xl, i + 1)
                    z_heads(0, 0).then_inc(f_z1, 1)
                    after(pe, f_mix, i + 1)
                    after(pe, f_pje, i + 1)
                    for h4 in range(4):
                        for e4 in range(4):
                            o = ps[32 * e4:32 * e4 + 32, 3, 0:P].rearrange("p (q a h) -> p q a h", q=NQ, a=2)
                            first = 8 * (h4 % 2) + h4 // 2
                            last = pe.matmul(o[:, :, :, first:first + 7:2], ident[:, 32 * h4:32 * h4 + 32],
                                             mix[:, :, :, e4::4].rearrange("p q n a -> p q a n"), start=True, stop=True)
                    last.then_inc(f_tr, 1)
                if back:
                    after(pe, f_vte, i)
                    after(pe, f_ae, i - 1)
                    for k in range(8):
                        last = pe.transpose(ps[:, 4 + k // 4, P * (k % 4):P * (k % 4) + P],
                                            vT[:, k, :, :].rearrange("p b t -> p (b t)"), ident[:, :])
                    last.then_inc(f_vv, 1)
                if front:
                    after(pe, f_ge, i + 1)
                    after(pe, f_tre, i + 1)
                    z_heads(8, 2).then_inc(f_z2, 1)
                if back:
                    after(pe, f_ete, 2 * i)
                    after(pe, f_vve, i)
                    for b in range(2):
                        for half in range(2):
                            for hg in range(HG):
                                for h4 in range(4):
                                    last = pe.matmul(ps[32 * h4:32 * h4 + 32, 6 + b, 256 * half + 64 * hg:256 * half + 64 * hg + 64],
                                                     eT[:, b, HG * half + hg, 32 * h4:32 * h4 + 32],
                                                     v_sb[:, 4 * hg + h4, :], start=True, stop=True)
                        last.then_inc(f_pv, 1)
                if front:
                    after(pe, f_z1e, i + 1)
                    after(pe, f_z2e, i + 1)
                    for q in range(NQ):
                        b = q // 2
                        for h4 in range(4):
                            last = pe.matmul(ps[32 * h4:32 * h4 + 32, b, 224 * (q % 2):224 * (q % 2) + 224].rearrange("p (n j) -> p n j", j=S),
                                             xnT[:, HALF * q:HALF * q + 32], z[:, h4::4, S * b:S * b + S], start=True, stop=True)
                    last.then_inc(f_s, 1)
                if nxt:
                    xn_turn(i + 1)
                if back:
                    after(pe, f_dm, i)
                    for q in range(NQ):
                        if q % 2 == 0:
                            after(pe, f_alo, 2 * i - 1 + q // 2)
                        for hg in range(HG):
                            n = HG * q + hg
                            last = pe.matmul(ps[:, 4 + q // 2, 224 * (q % 2):224 * (q % 2) + 224], ah[:, n, :, :].rearrange("p a d -> p (a d)"),
                                             dm[:, n, :, :].rearrange("p t e -> p (t e)"), start=(hg == 0), stop=(hg == HG - 1))
                    last.then_inc(f_a, 1)
                if nxt:
                    gates(i + 1)
                if back:
                    after(pe, f_ae, i)
                    if front:
                        after(pe, f_z2e, i + 1)
                    for e in range(E):
                        last = pe.matmul(ps[:, 3, 0:C], aT[:, e, :, :].rearrange("p b t -> p (b t)"), wo2[:, e, :],
                                         start=(e == 0), stop=(e == E - 1))
                    last.then_inc(f_o, 1)
                if front:
                    after(pe, f_e, i + 1)
                    after(pe, f_sub, i + 1)
                    for k in range(K16):
                        last = pe.transpose(ps[:, k // 4, P * (k % 4):P * (k % 4) + P],
                                            e_sb[:, k, :, :].rearrange("p b j -> p (b j)"), ident[:, :])
                    last.then_inc(f_et, 1)

            pe.wait_ge(mvd, NP)
            pe.wait_ge(fp_act, 5)
            pe.wait_ge(fp_dve, 2)
            xn_turn(0)
            gates(0)
            iteration(0, back=False)
            iteration(1)
            with pe.Fori(2, NP - 1) as i:
                iteration(i)
            iteration(NP - 1, nxt=False)
            iteration(NP, front=False, nxt=False)


_INS = ['x', 'ctx_1024', 'L0_xattn_Wq', 'L0_xattn_bq', 'L0_xattn_Wk', 'L0_xattn_bk', 'L0_xattn_Wv', 'L0_xattn_bv',
        'L0_ffn_Wq', 'L0_ffn_Wk', 'L0_ffn_Wv', 'L0_ffn_Ws', 'L0_ffn_Wd', 'L0_ffn_Wo']
_OUTS = [((32, 56, 128), 'float32')]


def kernel(**inputs):
    import numpy as _np
    import concourse.bacc as _bacc
    from concourse import mybir as _mybir
    from concourse.bass_utils import run_bass_kernel_spmd as _run

    nc = _bacc.Bacc("TRN2", target_bir_lowering=False, num_devices=1)
    arrays, args = {}, []
    for name in _INS:
        a = _np.ascontiguousarray(inputs[name])
        arrays[f"in_{name}_dram"] = a
        args.append(nc.dram_tensor(f"in_{name}_dram", a.shape, _mybir.dt.from_np(a.dtype), kind="ExternalInput").ap())
    for i, (shape, dtype) in enumerate(_OUTS):
        dt = _mybir.dt.from_np(_np.dtype(dtype))
        args.append(nc.dram_tensor(f"out_{i}_dram", shape, dt, kind="ExternalOutput").ap())
    xattn_ffn(nc, *args)
    r = _run(nc, [arrays], core_ids=[0])
    return r.results[0]["out_0_dram"]
```

```python
from contextlib import ExitStack

import concourse.bass as bass
from concourse import mybir

F32 = mybir.dt.float32
F16 = mybir.dt.float16
BF16 = mybir.dt.bfloat16
ALU = mybir.AluOpType
ACT = mybir.ActivationFunctionType
AX = mybir.AxisListType

P = 128
BANK = 512


def xattn_ffn(
    nc: bass.Bass,
    x: bass.AP,
    ctx: bass.AP,
    wq: bass.AP,
    bq: bass.AP,
    wk: bass.AP,
    bk: bass.AP,
    wv: bass.AP,
    bv: bass.AP,
    fwq: bass.AP,
    fwk: bass.AP,
    fwv: bass.AP,
    fws: bass.AP,
    fwd: bass.AP,
    fwo: bass.AP,
    out: bass.AP,
):
    B, S, C = x.shape
    L = ctx.shape[1]
    H, DH, _ = fwq.shape
    E = fwv.shape[0]
    assert C == P and S == 56 and H == 16 and DH == 64 and E == 8
    NP = B // 2
    SLOT = 64
    HALF = S // 2
    TK = -(-L // P)
    RPP = L // P
    REST = L - RPP * P
    DUP = P - REST
    EPS = 1e-5
    SCALE = float(DH) ** -0.5
    HG = H // 4
    NQ = 4
    K16 = 2 * HG
    MIX_UP, PJ_UP = 4096.0, 16.0
    DVE_K = 5

    x_v = x.rearrange("(p b) t c -> b t p c", b=2)

    es = ExitStack()
    with es:
        def sb(name, shape, dt=F32):
            return es.enter_context(nc.sbuf_tensor(name, shape, dt))

        def sem(name):
            return es.enter_context(nc.semaphore(name))

        ps = es.enter_context(nc.psum_tensor("ps", [P, 8, BANK], F32))

        ident = sb("ident", [P, P])
        ident16 = sb("ident16", [P, P], F16)
        diag_q = sb("diag_q", [P, S])
        ones16 = sb("ones16", [P, 1], F16)
        rows_of = sb("rows_of", [P, 2, P], BF16)
        diag_h = sb("diag_h", [P, HALF, H], F16)
        diag_e = sb("diag_e", [P, HALF, E], F16)
        rank = sb("rank", [P, 32, E], F16)

        x_all = sb("x_all", [P, NP * C])
        x2_all = sb("x2_all", [P, NP * C])
        y_all = sb("y_all", [P, NP * C])
        bv_all = sb("bv_all", [P, C])
        bq_col = sb("bq_col", [P, 1])
        bk_col = sb("bk_col", [P, 1])
        st_ve = sb("st_ve", [P, NP])
        st_std = sb("st_std", [P, NP])
        st_rstd = sb("st_rstd", [P, NP])

        wq_nat = sb("wq_nat", [P, C])
        wk_nat = sb("wk_nat", [P, C])
        wv_nat = sb("wv_nat", [P, C])
        wqT = sb("wqT", [P, C])
        wvT = sb("wvT", [P, C])
        xn1T = sb("xn1T", [P, B * S])
        qT = sb("qT", [P, B, SLOT])
        qk_all = sb("qk_all", [P, 2, B * S], F16)
        bk_rep = sb("bk_rep", [P, C])
        bkq = sb("bkq", [P, C + 1])
        cq_x = sb("cq_x", [P, NP])
        cq = sb("cq", [P, NP])

        ctxf_all = sb("ctxf_all", [P, 4 * TK * C])
        ctxf = [ctxf_all[:, TK * C * k:TK * C * (k + 1)] for k in range(4)]
        nat = [sb(f"nat{k}", [P, 2, TK * C], F16) for k in range(4)]
        ctxT = [sb(f"ctxT{b}", [P, 2 * TK * P], F16) for b in range(2)]
        qk_cur = [sb(f"qk_cur{s}", [P, 2, 2 * S], F16) for s in range(2)]
        tmax = sb("tmax", [P, 2, SLOT])
        m_q = sb("m_q", [P, 1])
        nshift = sb("nshift", [P, 1])
        dg = sb("dg", [P, 2, S], BF16)
        pf = [sb(f"pf{b}", [P, TK, S]) for b in range(2)]
        p16 = sb("p16", [P, 2, TK, 2, SLOT], F16)
        rden = sb("rden", [P, 1])
        aoT = sb("aoT", [P, 2, SLOT])
        bst = sb("bst", [P, 6])
        bst_all = sb("bst_all", [P, NP, 6])
        mv_all = sb("mv_all", [P, NP * 2])
        mv_cur = sb("mv_cur", [P, 2])
        x2_cur = sb("x2_cur", [P, C])

        fwq_nat = sb("fwq_nat", [P, H // 2, C])
        fwk_nat = sb("fwk_nat", [P, H // 2, C])
        fwv_nat = sb("fwv_nat", [P, E // 2, C])
        fws_nat = sb("fws_nat", [P, C])
        fwd_nat = sb("fwd_nat", [P, C])
        fwo_nat = sb("fwo_nat", [P, E, 2, DH])
        mT = sb("mT", [P, 2, H, C], F16)
        wg = sb("wg", [P, 4, 2, HG, E])
        fwvT = sb("fwvT", [P, E, DH])
        wo2 = sb("wo2", [P, E, C])

        xn = sb("xn", [P, C])
        xnT = sb("xnT", [P, 2 * S + 4])
        xn16 = sb("xn16", [P, 2, 2 * S], F16)
        z = xn1T[:, :].rearrange("p (h n) -> p h n", h=H)
        g_sb = sb("g_sb", [P, 32, E])
        th = sb("th", [P, NQ * HG, E])
        sg = sb("sg", [P, NQ * HG, E])
        m1 = sb("m1", [P, 32])
        eq1 = sb("eq1", [P, 32, E], F16)
        r1 = sb("r1", [P, 32, E], F16)
        s1 = sb("s1", [P, 32], F16)
        oh1 = sb("oh1", [P, 32, E], F16)
        g2 = sb("g2", [P, 32, E])
        m2 = sb("m2", [P, 32])
        eq2 = sb("eq2", [P, 32, E], F16)
        r2 = sb("r2", [P, 32, E], F16)
        s2 = sb("s2", [P, 32], F16)
        oh2 = sb("oh2", [P, 32, E], F16)
        chosen = sb("chosen", [P, 2 * NQ * HG, E], F16)
        mix = sb("mix", [P, NQ, HG, E])
        mixf = sb("mixf", [P, NQ * 2, H])
        mixp = sb("mixp", [P, 2, NQ * 2, H], F16)
        n_dv, n_dm, n_pj = NQ * 2 * HALF * H, NQ * HG * HALF * E // 2, NQ * 2 * DH
        assert n_dv + n_dm + n_pj <= 4 * TK * C
        dv = ctxf_all[:, 0:n_dv].bitcast(F16).rearrange("p (s k t h) -> p s k t h", s=2, k=NQ * 2, h=H)
        dm = ctxf_all[:, n_dv:n_dv + n_dm].bitcast(F16).rearrange("p (k t e) -> p k t e", k=NQ * HG, e=E)
        pj = ctxf_all[:, n_dv + n_dm:n_dv + n_dm + n_pj].bitcast(F16).rearrange("p (s k d) -> p s k d", s=2, d=DH)
        pjf = sb("pjf", [P, NQ * 2, DH])
        smx = sb("smx", [P, 2 * K16])
        ssub = sb("ssub", [P, 2 * K16, S])
        e_sb = sb("e_sb", [P, K16, 2, SLOT])
        rs = sb("rs", [P, K16 * 2])
        rinv = sb("rinv", [P, K16 * 2])
        eT = sb("eT", [P, 2, K16, P])
        vT = sb("vT", [P, H // 2, 2, SLOT])
        v_sb = sb("v_sb", [P, H, DH])
        attnf = sb("attnf", [P, 2 * K16, DH])
        ah = sb("ah", [P, 2 * K16, 2, DH], F16)
        aT = sb("aT", [P, E, 2, SLOT])

        x_loaded = sem("x_loaded")
        weights_loaded = sem("weights_loaded")
        ffn_weights_loaded = sem("ffn_weights_loaded")
        ctx_loaded = [sem(f"ctx_loaded{k}") for k in range(4)]
        out_written = sem("out_written")
        memsets_done = sem("memsets_done")
        ident_ready = sem("ident_ready")
        consts_ready = sem("consts_ready")
        ln1_stats = sem("ln1_stats")
        ln1_moments = sem("ln1_moments")
        ln1_var = sem("ln1_var")
        ln1_rstd = sem("ln1_rstd")
        ln1_done = sem("ln1_done")
        bk_spread = sem("bk_spread")
        bk_products = sem("bk_products")
        bk_products_out = sem("bk_products_out")
        xn_bk_ready = sem("xn_bk_ready")
        cq_summed = sem("cq_summed")
        x_bv_ready = sem("x_bv_ready")
        ffn_w_product = sem("ffn_w_product")
        ffn_w_copied = sem("ffn_w_copied")
        ffn_w_low = sem("ffn_w_low")
        xn_high = sem("xn_high")
        xn_low = sem("xn_low")
        ln1_std = sem("ln1_std")
        setup_product = sem("setup_product")
        setup_copied = sem("setup_copied")
        qk_low_ready = sem("qk_low_ready")
        qk_copied = sem("qk_copied")
        ctx_high = sem("ctx_high")
        ctx_low = sem("ctx_low")
        ctx_low_rest = sem("ctx_low_rest")
        tiles_turned = sem("tiles_turned")
        tiles_copied_dve = sem("tiles_copied_dve")
        tiles_copied_act = sem("tiles_copied_act")
        scores_done = sem("scores_done")
        tile_max_done = sem("tile_max_done")
        max_turned = sem("max_turned")
        query_max_done = sem("query_max_done")
        shift_ready = sem("shift_ready")
        shift_high = sem("shift_high")
        shift_low = sem("shift_low")
        scores_shifted = sem("scores_shifted")
        exps_done = sem("exps_done")
        exps_low = sem("exps_low")
        values_done = sem("values_done")
        denominator_done = sem("denominator_done")
        denominator_inverted = sem("denominator_inverted")
        sums_copied = sem("sums_copied")
        projection_done = sem("projection_done")
        x2_done = sem("x2_done")
        x2_stats = sem("x2_stats")
        x2_moments_kept = sem("x2_moments_kept")
        x2_moments = sem("x2_moments")
        x2_kept = sem("x2_kept")
        ln2_var = sem("ln2_var")
        ln2_std = sem("ln2_std")
        ln2_rstd = sem("ln2_rstd")
        xn_ready = sem("xn_ready")
        xn_turned = sem("xn_turned")
        xnT_copied = sem("xnT_copied")
        gates_done = sem("gates_done")
        gates_copied = sem("gates_copied")
        tanh_done = sem("tanh_done")
        experts_done = sem("experts_done")
        experts_copied = sem("experts_copied")
        z_first_done = sem("z_first_done")
        z_second_done = sem("z_second_done")
        z_first_copied = sem("z_first_copied")
        z_second_copied = sem("z_second_copied")
        ffn_scores_done = sem("ffn_scores_done")
        ffn_max_done = sem("ffn_max_done")
        ffn_shifted = sem("ffn_shifted")
        ffn_exps_done = sem("ffn_exps_done")
        ffn_sums_done = sem("ffn_sums_done")
        ffn_sums_inverted = sem("ffn_sums_inverted")
        gates_read = sem("gates_read")
        chosen_ready = sem("chosen_ready")
        sigmoid_done = sem("sigmoid_done")
        mix_ready = sem("mix_ready")
        mix_moved = sem("mix_moved")
        mix_copied = sem("mix_copied")
        diagonals_dve = sem("diagonals_dve")
        diagonals_pool = sem("diagonals_pool")
        experts_low = sem("experts_low")
        mix_low = sem("mix_low")
        masks_ready = sem("masks_ready")
        exps_turned = sem("exps_turned")
        exps_turned_copied = sem("exps_turned_copied")
        mixed_done = sem("mixed_done")
        mixed_copied = sem("mixed_copied")
        mixed_turned = sem("mixed_turned")
        mixed_turned_copied = sem("mixed_turned_copied")
        attention_done = sem("attention_done")
        attention_normalised = sem("attention_normalised")
        attention_high = sem("attention_high")
        attention_low = sem("attention_low")
        masked_done = sem("masked_done")
        masked_copied = sem("masked_copied")
        output_done = sem("output_done")
        y_ready = sem("y_ready")
        top_step = [sem(f"top_step{n}") for n in range(10)]

        def after(eng, s, value):
            if not isinstance(value, int) or value > 0:
                eng.wait_ge(s, value)

        NW, NFW = 6, 7
        NG = 4
        GW = B * S // NG
        block = es.enter_context(nc.Block())

        @block.sync
        def _(sp):
            sp.wait_ge(memsets_done, 1)
            for b in range(2):
                sp.dma_start(x_all[SLOT * b:SLOT * b + S, :].rearrange("t (p c) -> t p c", c=C), x_v[b]).then_inc(x_loaded, 16)
            for dst, src in ((wq_nat[:, :], wq), (wk_nat[:, :], wk), (wv_nat[:, :], wv),
                             (bq_col[:, :], bq.rearrange("(d o) -> d o", o=1)), (bk_col[:, :], bk.rearrange("(d o) -> d o", o=1)),
                             (bv_all[:, :], bv.rearrange("(o d) -> o d", o=1).broadcast_to((P, C)))):
                sp.dma_start(dst, src).then_inc(weights_loaded, 16)

            def load(k, n):
                sp.dma_start(ctxf[k][:, 0:RPP * C], ctx[n, 0:RPP * P, :].rearrange("(p r) c -> p (r c)", r=RPP)).then_inc(ctx_loaded[k], 16)
                sp.dma_start(ctxf[k][0:REST, RPP * C:], ctx[n, RPP * P:L, :]).then_inc(ctx_loaded[k], 16)
                sp.dma_start(ctxf[k][REST:P, RPP * C:], ctx[n, L - DUP:L, :]).then_inc(ctx_loaded[k], 16)

            for k in range(4):
                load(k, k)
            for dst, src in (
                (fwq_nat[:, :, :], fwq.rearrange("(k h) d c -> (h d) k c", h=2)),
                (fwk_nat[:, :, :], fwk.rearrange("(k h) d c -> (h d) k c", h=2)),
                (fwv_nat[:, :, :], fwv.rearrange("(k e) d c -> (e d) k c", e=2)),
                (fws_nat[:, :], fws.rearrange("h e c -> (h e) c")),
                (fwd_nat[:, :], fwd.rearrange("h e c -> (h e) c")),
                (fwo_nat[:, :, 0, :], fwo.rearrange("e f d -> f e d")),
                (fwo_nat[:, :, 1, :], fwo.rearrange("e f d -> f e d")),
            ):
                sp.dma_start(dst, src).then_inc(ffn_weights_loaded, 16)

            def loads(i):
                for k in range(4):
                    n = 4 * i + k
                    after(sp, ctx_high, n - 3)
                    after(sp, ctx_low, n - 3)
                    after(sp, ctx_low_rest, n - 3)
                    sp_load(k, n)

            def sp_load(k, n):
                flat = ctx.rearrange("n l c -> (n l) c")
                sp.dma_start(ctxf[k][:, 0:RPP * C],
                             flat[bass.ds(n * L, RPP * P), :].rearrange("(p r) c -> p (r c)", r=RPP)).then_inc(ctx_loaded[k], 16)
                sp.dma_start(ctxf[k][0:REST, RPP * C:], flat[bass.ds(n * L + RPP * P, REST), :]).then_inc(ctx_loaded[k], 16)
                sp.dma_start(ctxf[k][REST:P, RPP * C:], flat[bass.ds(n * L + L - DUP, DUP), :]).then_inc(ctx_loaded[k], 16)

            with sp.Fori(1, NP // 2) as i:
                loads(i)
            with sp.Fori(0, NP) as i:
                after(sp, y_ready, i + 1)
                for b in range(2):
                    sp.dma_start(out.rearrange("n t c -> (n t) c")[bass.ds(i * (2 * S) + b * S, S), :],
                                 y_all[SLOT * b:SLOT * b + S, bass.ds(i * C, C)]).then_inc(out_written, 16)
            sp.wait_ge(out_written, 32 * NP)

        @block.gpsimd
        def _(pool):
            pool.memset(x_all[:, :], 0.0).then_inc(memsets_done, 1)
            pool.memset(ident[:, :], 0.0).then_inc(ident_ready, 1)
            pool.wait_ge(ident_ready, 1)
            pool.affine_select(out=ident[:, :], in_=ident[:, :], compare_op=ALU.not_equal, fill=1.0, base=0,
                               pattern=[[-1, P]], channel_multiplier=1).then_inc(ident_ready, 1)
            pool.memset(qT[:, :, :], 0.0).then_inc(memsets_done, 1)
            pool.memset(tmax[:, :, :], 0.0).then_inc(memsets_done, 1)
            pool.memset(p16[:, 0, :, :, :], 1.0).then_inc(memsets_done, 1)
            pool.memset(p16[:, 1, :, :, :], 0.0).then_inc(memsets_done, 1)
            pool.memset(aoT[:, :, :], 0.0).then_inc(memsets_done, 1)
            pool.memset(rows_of[:, :, :], 0.0).then_inc(memsets_done, 1)
            pool.memset(ones16[:, :], 1.0).then_inc(memsets_done, 1)
            pool.wait_ge(memsets_done, 8)
            for b in range(2):
                pool.memset(rows_of[SLOT * b:SLOT * b + SLOT, b, :], -1.0).then_inc(memsets_done, 1)
            pool.wait_ge(memsets_done, 10)
            for e in range(E):
                pool.memset(rank[:, :, e], float(E - e)).then_inc(memsets_done, 1)
            pool.memset(e_sb[:, :, :, :], 0.0).then_inc(memsets_done, 1)
            pool.memset(vT[:, :, :, :], 0.0).then_inc(memsets_done, 1)
            pool.memset(aT[:, :, :, :], 0.0).then_inc(memsets_done, 1)
            pool.memset(xnT[:, :], 0.0).then_inc(memsets_done, 1)
            pool.memset(eT[:, :, :, :], 0.0).then_inc(memsets_done, 1)

            def low_rows(n, k):
                after(pool, ctx_high, n + 1)
                pool.tensor_tensor(nat[k][:, 1, 7 * C:], ctxf[k][:, 7 * C:], nat[k][:, 0, 7 * C:], ALU.subtract).then_inc(ctx_low_rest, 1)

            def low_probs(n, b, pair):
                after(pool, exps_done, 2 * n + 2)
                after(pool, denominator_done, pair)
                pool.tensor_tensor(p16[:, 1, :, b, 0:S], pf[b][:, :, :], p16[:, 0, :, b, 0:S], ALU.subtract).then_inc(exps_low, 1)

            def keep(pair):
                after(pool, x2_done, pair + 1)
                pool.tensor_copy(x2_all[:, bass.ds(pair * C, C)], x2_cur[:, :]).then_inc(x2_kept, 1)

            def queries(pair, s):
                after(pool, scores_done, 2 * pair - 2)
                pool.tensor_copy(qk_cur[s][:, :, :], qk_all[:, :, bass.ds(pair * (2 * S), 2 * S)]).then_inc(qk_copied, 1)

            def steps(i):
                for s in range(2):
                    pair = 2 * i + s
                    n = 2 * pair
                    first = isinstance(pair, int) and pair == 0
                    more = not (isinstance(pair, int) and pair == NP - 1)
                    if more:
                        low_rows(n + 2, (2 * s + 2) % 4)
                        low_rows(n + 3, (2 * s + 3) % 4)
                        queries(pair + 1, 1 - s)
                    low_probs(n, 0, pair)
                    low_probs(n + 1, 1, pair)
                    if not first:
                        keep(pair - 1)

            pool.wait_ge(bk_products_out, 1)
            pool.wait_ge(ln1_done, NG)
            pool.tensor_tensor(x2_all[:, :].rearrange("p (n c) -> p n c", c=C), y_all[:, :].rearrange("p (n c) -> p n c", c=C),
                               bkq[:, 0:C].unsqueeze(1).broadcast_to((P, NP, C)), ALU.mult).then_inc(xn_bk_ready, 1)
            low_rows(0, 0)
            low_rows(1, 1)
            pool.wait_ge(qk_low_ready, NG)
            queries(0, 0)
            steps(0)
            with pool.Fori(1, NP // 2 - 1) as i:
                steps(i)
            steps(NP // 2 - 1)
            keep(NP - 1)

            def masks(i):
                after(pool, chosen_ready, i + 1)
                after(pool, masked_done, i)
                pool.tensor_tensor(dm[:, :, :, :], chosen[:, NQ * HG:, :].unsqueeze(2).broadcast_to((P, NQ * HG, HALF, E)),
                                   diag_e[:, :, :].unsqueeze(1).broadcast_to((P, NQ * HG, HALF, E)), ALU.mult).then_inc(masks_ready, 1)

            def low_tokens(i):
                after(pool, xnT_copied, i + 1)
                after(pool, xn_high, i + 1)
                pool.tensor_tensor(xn16[:, 1, :], xnT[:, 0:2 * S], xn16[:, 0, :], ALU.subtract).then_inc(xn_low, 1)

            def weights(i):
                after(pool, mix_copied, i + 1)
                after(pool, mixed_done, i)
                n = 2 * NQ - DVE_K
                for part in range(2):
                    if part == 1:
                        after(pool, mix_low, i + 1)
                    last = pool.tensor_tensor(dv[:, part, DVE_K:, :, :],
                                              mixp[:, part, DVE_K:, :].unsqueeze(2).broadcast_to((P, n, HALF, H)),
                                              diag_h[:, :, :].unsqueeze(1).broadcast_to((P, n, HALF, H)), ALU.mult)
                last.then_inc(diagonals_pool, 1)

            def low_experts(i):
                after(pool, experts_copied, i + 1)
                after(pool, mixed_done, i)
                pool.tensor_tensor(pj[:, 1, :, :], pjf[:, :, :], pj[:, 0, :, :], ALU.subtract).then_inc(experts_low, 1)

            def after_choice(i, nxt=True):
                low_experts(i)
                weights(i)
                if nxt:
                    low_tokens(i + 1)
                masks(i)

            pool.wait_ge(consts_ready, 11)
            pool.wait_ge(x2_moments_kept, NP)
            low_tokens(0)
            after_choice(0)
            with pool.Fori(1, NP - 1) as i:
                after_choice(i)
            after_choice(NP - 1, nxt=False)

        @block.scalar
        def _(act):
            act.wait_ge(setup_product, 1)
            act.copy(wqT[:, :], ps[:, 0, 0:P])
            act.copy(wvT[:, :], ps[:, 0, P:2 * P]).then_inc(setup_copied, 1)
            for g in range(NG):
                act.wait_ge(ln1_var, g + 1)
                act.sqrt(st_std[:, 4 * g:4 * g + 4], st_ve[:, 4 * g:4 * g + 4]).then_inc(ln1_std, 1)
            for g in range(NG):
                act.wait_ge(setup_product, 2 + g)
                act.copy(xn1T[:, GW * g:GW * (g + 1)].rearrange("p (n t) -> p n t", t=S),
                         ps[:, (5, 6, 7, 0)[g], :].rearrange("p (n t) -> p n t", t=SLOT)[:, :, 0:S]).then_inc(setup_copied, 1)
            act.wait_ge(memsets_done, 2)
            for g in range(NG):
                act.wait_ge(setup_product, 2 + NG + g)
                act.activation(qT[:, 8 * g:8 * g + 8, 0:S], ps[:, 1 + g, 0:GW].rearrange("p (n t) -> p n t", t=S),
                               ACT.Identity, bias=bq_col[:, 0:1]).then_inc(setup_copied, 1)
            for g in range(NG):
                act.wait_ge(setup_product, 2 + 2 * NG + g)
                act.copy(qk_all[:, 0, GW * g:GW * (g + 1)], ps[:, (5, 6, 7, 0)[g], 0:GW]).then_inc(setup_copied, 1)

            def split_hi(n, k, turn):
                act.wait_ge(ctx_loaded[k], 48 * (turn + 1))
                after(act, values_done, n - 3)
                act.copy(nat[k][:, 0, :], ctxf[k][:, :]).then_inc(ctx_high, 1)

            def t_evac(n, b):
                after(act, tiles_turned, 3 * n + 2)
                after(act, scores_done, n - 1)
                act.copy(ctxT[b][:, 8 * P:16 * P], ps[:, (3 * b + 1) % 2, :].bitcast(F16)).then_inc(tiles_copied_act, 1)

            def exps(n, b, pair):
                after(act, scores_shifted, n + 1)
                after(act, denominator_done, pair)
                act.activation(p16[:, 0, :, b, 0:S].rearrange("p (a t) q -> p a t q", a=2),
                               ps[:, 2 + 2 * b:4 + 2 * b, 0:6 * S].rearrange("p a (t q) -> p a t q", t=6), ACT.Exp).then_inc(exps_done, 1)
                act.activation(pf[b][:, :, :].rearrange("p (a t) q -> p a (t q)", a=2),
                               ps[:, 2 + 2 * b:4 + 2 * b, 0:6 * S], ACT.Exp).then_inc(exps_done, 1)

            def steps(i):
                for s in range(2):
                    pair = 2 * i + s
                    n = 2 * pair
                    more = not (isinstance(pair, int) and pair == NP - 1)
                    if more:
                        split_hi(n + 2, (2 * s + 2) % 4, i + s)
                        split_hi(n + 3, (2 * s + 3) % 4, i + s)
                        t_evac(n + 2, 0)
                    exps(n, 0, pair)
                    exps(n + 1, 1, pair)
                    if more:
                        t_evac(n + 3, 1)

            split_hi(0, 0, 0)
            split_hi(1, 1, 0)
            t_evac(0, 0)
            t_evac(1, 1)
            act.wait_ge(memsets_done, 5)
            steps(0)
            with act.Fori(1, NP // 2 - 1) as i:
                steps(i)
            steps(NP // 2 - 1)

            act.wait_ge(ffn_w_product, 1)
            act.copy(fwvT[:, :, :], ps[:, 0, :].rearrange("p (e d) -> p e d", e=E)).then_inc(ffn_w_copied, 1)
            act.wait_ge(ffn_w_product, 2)
            for g in range(2):
                last = act.copy(wg[:, :, g, :, :].rearrange("p a b e -> p b a e"),
                                ps[:, 1, P * g:P * g + P].rearrange("p (b a e) -> p b a e", b=HG, a=4))
            last.then_inc(ffn_w_copied, 1)
            act.wait_ge(ffn_w_product, 3)
            act.copy(wo2[:, :, :], ps[:, 2:4, :].rearrange("p a (e f) -> p (a e) f", f=C)).then_inc(ffn_w_copied, 1)
            mT_v = mT[:, 0, :, :].rearrange("p (a k h) c -> p h a k c", a=2, h=2)
            for h2 in range(2):
                act.wait_ge(ffn_w_product, 4 + h2)
                for a in range(2):
                    last = act.copy(mT_v[:, h2, a, :, :], ps[:, 4 * h2 + a, :].rearrange("p (k c) -> p k c", c=C))
                last.then_inc(ffn_w_copied, 1)
            act.wait_ge(ln2_var, 1)
            act.sqrt(st_std[:, :], st_ve[:, :]).then_inc(ln2_std, 1)

            def xnT_evac(i):
                after(act, xn_turned, i + 1)
                after(act, ffn_scores_done, i)
                act.copy(xnT[:, 0:2 * S].rearrange("p (b t) -> p b t", b=2),
                         ps[:, 2, 0:P].rearrange("p (b t) -> p b t", b=2)[:, :, 0:S]).then_inc(xnT_copied, 1)
                act.copy(xn16[:, 0, :].rearrange("p (b t) -> p b t", b=2),
                         ps[:, 2, 0:P].rearrange("p (b t) -> p b t", b=2)[:, :, 0:S]).then_inc(xn_high, 1)

            def gates_out(i):
                after(act, gates_done, i + 1)
                after(act, gates_read, i)
                act.copy(g_sb[:, :, :].rearrange("p (g q n) e -> p q g (n e)", g=2, q=NQ),
                         ps[:, 2, 0:2 * P].rearrange("p (q g m) -> p q g m", q=NQ, g=2)).then_inc(gates_copied, 1)
                act.wait_ge(gates_copied, i + 1)
                after(act, sigmoid_done, i)
                act.activation(th[:, :, :], g_sb[:, 0:16, :], ACT.Tanh, scale=0.5).then_inc(tanh_done, 1)

            def iteration(i, front=True, back=True, nxt=True):
                if back:
                    after(act, mixed_done, i)
                    after(act, mixed_turned, i - 1)
                    act.mul(vT[:, :, :, 0:S].rearrange("p h b t -> p b t h"),
                            ps[:, 6:8, 0:8 * S].rearrange("p b (t h) -> p b t h", h=8), 1.0 / (MIX_UP * PJ_UP)).then_inc(mixed_copied, 1)
                if front:
                    after(act, experts_done, i + 1)
                    after(act, mixed_done, i)
                    after(act, experts_low, i)
                    act.mul(pjf[:, :, :], ps[:, 3, :].rearrange("p (q d) -> p q d", d=DH), PJ_UP)
                    act.mul(pj[:, 0, :, :], ps[:, 3, :].rearrange("p (q d) -> p q d", d=DH), PJ_UP).then_inc(experts_copied, 1)
                    after(act, z_first_done, i + 1)
                    after(act, ffn_scores_done, i)
                    act.mul(z[:, 0:8, :].rearrange("p (a k) n -> p a (k n)", a=2), ps[:, 0:2, 0:8 * S], SCALE).then_inc(z_first_copied, 1)
                    after(act, mix_moved, i + 1)
                    after(act, diagonals_dve, i)
                    after(act, diagonals_pool, i)
                    act.mul(mixp[:, 0, :, :], ps[:, 3, 0:P].rearrange("p (q h) -> p q h", h=H), MIX_UP)
                    act.mul(mixf[:, :, :], ps[:, 3, 0:P].rearrange("p (q h) -> p q h", h=H), MIX_UP).then_inc(mix_copied, 1)
                if back:
                    after(act, mixed_turned, i)
                    after(act, attention_done, 2 * i - 2)
                    act.copy(v_sb[:, :, :].rearrange("p (a h) d -> p a (h d)", a=2), ps[:, 4:6, :]).then_inc(mixed_turned_copied, 1)
                if front:
                    after(act, z_second_done, i + 1)
                    after(act, ffn_scores_done, i)
                    act.mul(z[:, 8:16, :].rearrange("p (a k) n -> p a (k n)", a=2), ps[:, 2:4, 0:8 * S], SCALE).then_inc(z_second_copied, 1)
                if nxt:
                    xnT_evac(i + 1)
                if back:
                    after(act, masked_done, i)
                    after(act, output_done, i - 1)
                    act.copy(aT[:, :, :, 0:S].rearrange("p e b t -> p b t e"),
                             ps[:, 4:6, 0:8 * S].rearrange("p b (t e) -> p b t e", e=E)).then_inc(masked_copied, 1)
                if front:
                    after(act, ffn_shifted, i + 1)
                    after(act, exps_turned, i)
                    after(act, ffn_sums_done, i)
                    act.activation(e_sb[:, :, :, 0:S].rearrange("p k b j -> p b k j"),
                                   ssub[:, :, :].rearrange("p (b k) j -> p b k j", b=2), ACT.Exp).then_inc(ffn_exps_done, 1)
                if nxt:
                    gates_out(i + 1)
                if front:
                    after(act, exps_turned, i + 1)
                    after(act, attention_done, 2 * i)
                    for b in range(2):
                        r = slice(SLOT * b, SLOT * b + SLOT)
                        act.copy(eT[r, b, :, :].rearrange("p (a k) n -> p a (k n)", a=2), ps[r, 0:2, :]).then_inc(exps_turned_copied, 1)

            act.wait_ge(memsets_done, 23)
            xnT_evac(0)
            gates_out(0)
            iteration(0, back=False)
            iteration(1)
            with act.Fori(2, NP - 1) as i:
                iteration(i)
            iteration(NP - 1, nxt=False)
            iteration(NP, front=False, nxt=False)

        @block.vector
        def _(dve):
            v3 = lambda t: t[:, :].rearrange("p (n c) -> p n c", c=C)
            dve.wait_ge(ident_ready, 2)
            dve.tensor_copy(ident16[:, :], ident[:, :]).then_inc(consts_ready, 1)
            for b in range(2):
                dve.tensor_copy(diag_q[SLOT * b:SLOT * b + SLOT, :], ident[SLOT * b:SLOT * b + SLOT, SLOT * b:SLOT * b + S]).then_inc(consts_ready, 1)
            dve.wait_ge(weights_loaded, 16 * NW)
            dve.tensor_copy(bk_rep[:, :], bk_col[:, 0:1].broadcast_to((P, C))).then_inc(bk_spread, 1)
            dve.wait_ge(x_loaded, 32)

            def ln_stats(g):
                for n in range(4 * g, 4 * g + 4):
                    last = dve.bn_stats(bst_all[:, n, :], x_all[:, C * n:C * n + C])
                last.then_inc(ln1_stats, 1)
                dve.wait_ge(ln1_stats, g + 1)
                for n in range(4 * g, 4 * g + 4):
                    last = dve.bn_aggr(mv_all[:, 2 * n:2 * n + 2], bst_all[:, n, :])
                last.then_inc(ln1_moments, 1)
                dve.wait_ge(ln1_moments, g + 1)
                dve.tensor_scalar(st_ve[:, 4 * g:4 * g + 4], mv_all[:, :].rearrange("p (n k) -> p n k", k=2)[:, 4 * g:4 * g + 4, 1],
                                  EPS, None, ALU.add).then_inc(ln1_var, 1)

            def ln_apply(g):
                dve.wait_ge(ln1_std, g + 1)
                dve.reciprocal(st_rstd[:, 4 * g:4 * g + 4], st_std[:, 4 * g:4 * g + 4]).then_inc(ln1_rstd, 1)
                dve.wait_ge(ln1_rstd, g + 1)
                for n in range(4 * g, 4 * g + 4):
                    last = dve.tensor_scalar(y_all[:, C * n:C * n + C], x_all[:, C * n:C * n + C], mv_all[:, 2 * n:2 * n + 1],
                                             st_rstd[:, n:n + 1], ALU.subtract, ALU.mult)
                last.then_inc(ln1_done, 1)

            dve.wait_ge(bk_products, 1)
            dve.tensor_copy(bkq[:, :], ps[:, 1, 0:C + 1]).then_inc(bk_products_out, 1)
            ln_stats(0)
            for g in range(NG):
                if g + 1 < NG:
                    ln_stats(g + 1)
                ln_apply(g)
            dve.wait_ge(ln1_done, NG)
            dve.tensor_tensor(v3(x_all), v3(x_all), bv_all[:, :].unsqueeze(1).broadcast_to((P, NP, C)), ALU.add).then_inc(x_bv_ready, 1)
            for q in range(4):
                r = slice(32 * q, 32 * q + 32)
                cut = ident[r, 32 * q:32 * q + HALF].unsqueeze(2)
                dve.tensor_copy(diag_h[r, :, :], cut.broadcast_to((32, HALF, H))).then_inc(consts_ready, 1)
                dve.tensor_copy(diag_e[r, :, :], cut.broadcast_to((32, HALF, E))).then_inc(consts_ready, 1)
            for g in range(NG):
                dve.wait_ge(setup_copied, 2 + 2 * NG + g)
                dve.tensor_tensor(qk_all[:, 1, GW * g:GW * (g + 1)], ps[:, (5, 6, 7, 0)[g], 0:GW],
                                  qk_all[:, 0, GW * g:GW * (g + 1)], ALU.subtract).then_inc(qk_low_ready, 1)

            def split_lo(n, k):
                after(dve, ctx_high, n + 1)
                dve.tensor_tensor(nat[k][:, 1, 0:7 * C], ctxf[k][:, 0:7 * C], nat[k][:, 0, 0:7 * C],
                                  ALU.subtract).then_inc(ctx_low, 1)

            def t_evac(n, b, c):
                after(dve, tiles_turned, 3 * n + c + 1)
                after(dve, scores_done, n - 1)
                dve.tensor_copy(ctxT[b][:, 8 * P * c:8 * P * (c + 1)], ps[:, (3 * b + c) % 2, :].bitcast(F16)).then_inc(tiles_copied_dve, 1)

            def tile_max(n, pair, b):
                after(dve, scores_done, n + 1)
                after(dve, max_turned, pair)
                dve.tensor_reduce(tmax[:, b, 0:S], ps[:, 2 + 2 * b:4 + 2 * b, 0:6 * S].rearrange("p a (t q) -> p q a t", t=6),
                                  AX.XY, ALU.max).then_inc(tile_max_done, 1)

            def shifts(pair):
                after(dve, max_turned, pair + 1)
                dve.tensor_reduce(m_q[:, :], ps[:, 7, 0:P], AX.X, ALU.max).then_inc(query_max_done, 1)
                dve.wait_ge(query_max_done, pair + 1)
                dve.scalar_tensor_tensor(nshift[:, :], m_q[:, :], cq[:, bass.ds(pair, 1)], cq[:, bass.ds(pair, 1)],
                                         op0=ALU.add, op1=ALU.subtract).then_inc(shift_ready, 1)
                dve.wait_ge(shift_ready, pair + 1)
                after(dve, scores_shifted, 2 * pair)
                dve.tensor_scalar(dg[:, 0, :], diag_q[:, :], nshift[:, 0:1], None, ALU.mult).then_inc(shift_high, 1)
                dve.wait_ge(shift_high, pair + 1)
                dve.scalar_tensor_tensor(dg[:, 1, :], diag_q[:, :], nshift[:, 0:1], dg[:, 0, :],
                                         op0=ALU.mult, op1=ALU.subtract).then_inc(shift_low, 1)

            def sums_out(pair):
                after(dve, values_done, 2 * pair + 2)
                after(dve, denominator_done, pair + 1)
                after(dve, projection_done, pair)
                dve.tensor_copy(aoT[:, :, 0:S], ps[:, 6, 0:P].rearrange("p (b q) -> p b q", b=2)[:, :, 0:S]).then_inc(sums_copied, 1)

            def den_out(pair):
                dve.reciprocal(rden[:, :], ps[:, 6, P:P + 1]).then_inc(denominator_inverted, 1)

            def result(pair):
                after(dve, denominator_inverted, pair + 1)
                after(dve, x2_kept, pair)
                after(dve, projection_done, pair + 1)
                dve.scalar_tensor_tensor(x2_cur[:, :], ps[:, 6, 2 * P:3 * P], rden[:, 0:1],
                                         x_all[:, bass.ds(pair * C, C)], op0=ALU.mult, op1=ALU.add).then_inc(x2_done, 1)

            def moments(pair):
                dve.wait_ge(x2_done, pair + 1)
                dve.bn_stats(bst[:, :], x2_cur[:, :]).then_inc(x2_stats, 1)
                dve.wait_ge(memsets_done, 6)
                dve.wait_ge(x2_stats, pair + 1)
                dve.bn_aggr(mv_cur[:, :], bst[:, :]).then_inc(x2_moments, 1)
                dve.wait_ge(x2_moments, pair + 1)
                dve.tensor_copy(mv_all[:, bass.ds(pair * 2, 2)], mv_cur[:, :]).then_inc(x2_moments_kept, 1)

            def steps(i):
                for s in range(2):
                    pair = 2 * i + s
                    n = 2 * pair
                    first = isinstance(pair, int) and pair == 0
                    more = not (isinstance(pair, int) and pair == NP - 1)
                    tile_max(n, pair, 0)
                    tile_max(n + 1, pair, 1)
                    shifts(pair)
                    if more:
                        split_lo(n + 2, (2 * s + 2) % 4)
                    if not first:
                        sums_out(pair - 1)
                    if more:
                        t_evac(n + 2, 0, 0)
                    if not first:
                        den_out(pair - 1)
                    if more:
                        split_lo(n + 3, (2 * s + 3) % 4)
                        t_evac(n + 2, 0, 2)
                        t_evac(n + 3, 1, 0)
                    if not first:
                        result(pair - 1)
                        moments(pair - 1)
                    if more:
                        t_evac(n + 3, 1, 2)

            for b in range(2):
                split_lo(b, b)
            for b in range(2):
                t_evac(b, b, 0)
                t_evac(b, b, 2)
            dve.wait_ge(xn_bk_ready, 1)
            dve.tensor_reduce(cq_x[:, :], v3(x2_all), AX.X, ALU.add).then_inc(cq_summed, 1)
            dve.wait_ge(cq_summed, 1)
            dve.tensor_scalar(cq[:, :], cq_x[:, :], bkq[:, C:C + 1], None, ALU.add).then_inc(qk_low_ready, 1)
            dve.wait_ge(memsets_done, 6)
            dve.wait_ge(x_bv_ready, 1)
            dve.wait_ge(qk_low_ready, NG + 1)
            steps(0)
            with dve.Fori(1, NP // 2 - 1) as i:
                steps(i)
            steps(NP // 2 - 1)
            sums_out(NP - 1)
            den_out(NP - 1)
            result(NP - 1)
            moments(NP - 1)

            mT_v = mT[:, :, :, :].rearrange("p s (a k h) c -> p s h a k c", a=2, h=2)
            for h2 in range(2):
                dve.wait_ge(ffn_w_copied, 4 + h2)
                for a in range(2):
                    last = dve.tensor_tensor(mT_v[:, 1, h2, a, :, :], ps[:, 4 * h2 + a, :].rearrange("p (k c) -> p k c", c=C),
                                             mT_v[:, 0, h2, a, :, :], ALU.subtract)
                last.then_inc(ffn_w_low, 1)
            dve.wait_ge(x2_moments_kept, NP)
            dve.tensor_scalar(st_ve[:, :], mv_all[:, :].rearrange("p (n k) -> p n k", k=2)[:, :, 1], EPS, None, ALU.add).then_inc(ln2_var, 1)
            dve.wait_ge(ln2_std, 1)
            dve.reciprocal(st_rstd[:, :], st_std[:, :]).then_inc(ln2_rstd, 1)
            dve.wait_ge(ln2_rstd, 1)

            def normalise(i):
                after(dve, xn_turned, i)
                dve.tensor_scalar(xn[:, :], x2_all[:, bass.ds(i * C, C)], mv_all[:, bass.ds(i * 2, 1)],
                                  st_rstd[:, bass.ds(i, 1)], ALU.subtract, ALU.mult).then_inc(xn_ready, 1)

            per8 = lambda t: t[:, :].unsqueeze(2).broadcast_to((P, 32, E))

            def top_two(i):
                after(dve, gates_copied, i + 1)
                dve.tensor_reduce(m1[:, :], g_sb[:, :, :], AX.X, ALU.max).then_inc(top_step[0], 1)
                dve.wait_ge(top_step[0], i + 1)
                dve.tensor_tensor(eq1[:, :, :], g_sb[:, :, :], per8(m1), ALU.is_equal).then_inc(top_step[1], 1)
                dve.wait_ge(top_step[1], i + 1)
                dve.tensor_tensor(r1[:, :, :], eq1[:, :, :], rank[:, :, :], ALU.mult).then_inc(top_step[2], 1)
                dve.wait_ge(top_step[2], i + 1)
                dve.tensor_reduce(s1[:, :], r1[:, :, :], AX.X, ALU.max).then_inc(top_step[3], 1)
                dve.wait_ge(top_step[3], i + 1)
                dve.tensor_tensor(oh1[:, :, :], r1[:, :, :], per8(s1), ALU.is_equal).then_inc(top_step[4], 1)
                dve.wait_ge(top_step[4], i + 1)
                dve.scalar_tensor_tensor(g2[:, :, :], oh1[:, :, :], -3.0e38, g_sb[:, :, :], op0=ALU.mult, op1=ALU.add).then_inc(gates_read, 1)

            def second(i):
                dve.wait_ge(gates_read, i + 1)
                dve.tensor_reduce(m2[:, :], g2[:, :, :], AX.X, ALU.max).then_inc(top_step[5], 1)
                dve.wait_ge(top_step[5], i + 1)
                dve.tensor_tensor(eq2[:, :, :], g2[:, :, :], per8(m2), ALU.is_equal).then_inc(top_step[6], 1)
                dve.wait_ge(top_step[6], i + 1)
                dve.tensor_tensor(r2[:, :, :], eq2[:, :, :], rank[:, :, :], ALU.mult).then_inc(top_step[7], 1)
                dve.wait_ge(top_step[7], i + 1)
                dve.tensor_reduce(s2[:, :], r2[:, :, :], AX.X, ALU.max).then_inc(top_step[8], 1)
                dve.wait_ge(top_step[8], i + 1)
                dve.tensor_tensor(oh2[:, :, :], r2[:, :, :], per8(s2), ALU.is_equal).then_inc(top_step[9], 1)
                dve.wait_ge(top_step[9], i + 1)
                after(dve, masks_ready, i)
                dve.tensor_tensor(chosen[:, :, :], oh1[:, :, :], oh2[:, :, :], ALU.add).then_inc(chosen_ready, 1)

            def mixing(i):
                after(dve, tanh_done, i + 1)
                dve.tensor_scalar(sg[:, :, :], th[:, :, :], 0.5, 0.5, ALU.mult, ALU.add).then_inc(sigmoid_done, 1)
                dve.wait_ge(sigmoid_done, i + 1)
                dve.wait_ge(chosen_ready, i + 1)
                after(dve, mix_moved, i)
                dve.tensor_tensor(mix[:, :, :, :].rearrange("p q n e -> p (q n) e"), sg[:, :, :], chosen[:, 0:NQ * HG, :],
                                  ALU.mult).then_inc(mix_ready, 1)

            def iteration(i, front=True, back=True, nxt=True):
                if front:
                    mixing(i)
                if nxt:
                    normalise(i + 1)
                if back:
                    after(dve, ffn_exps_done, i)
                    dve.tensor_reduce(rs[:, :], e_sb[:, :, :, :].rearrange("p k b j -> p (k b) j"), AX.X, ALU.add).then_inc(ffn_sums_done, 1)
                    dve.wait_ge(ffn_sums_done, i)
                    dve.reciprocal(rinv[:, :], rs[:, :]).then_inc(ffn_sums_inverted, 1)
                if front:
                    after(dve, mix_copied, i + 1)
                    after(dve, mixed_done, i)
                    dve.tensor_tensor(mixp[:, 1, :, :], mixf[:, :, :], mixp[:, 0, :, :], ALU.subtract).then_inc(mix_low, 1)
                    dve.wait_ge(mix_low, i + 1)
                    for part in range(2):
                        last = dve.tensor_tensor(dv[:, part, 0:DVE_K, :, :],
                                                 mixp[:, part, 0:DVE_K, :].unsqueeze(2).broadcast_to((P, DVE_K, HALF, H)),
                                                 diag_h[:, :, :].unsqueeze(1).broadcast_to((P, DVE_K, HALF, H)), ALU.mult)
                    last.then_inc(diagonals_dve, 1)
                if back:
                    after(dve, ffn_sums_inverted, i)
                    after(dve, masked_done, i - 1)
                    for b in range(2):
                        k = slice(K16 * b, K16 * b + K16)
                        after(dve, attention_done, 2 * i - 1 + b)
                        dve.tensor_tensor(attnf[:, k, :], ps[:, 6 + b, :].rearrange("p (k d) -> p k d", d=DH),
                                          rinv[:, :].rearrange("p (k b) -> p b k", b=2)[:, b, :].unsqueeze(2).broadcast_to((P, K16, DH)),
                                          ALU.mult).then_inc(attention_normalised, 1)
                        dve.wait_ge(attention_normalised, 2 * i - 1 + b)
                        dve.tensor_copy(ah[:, k, 0, :], attnf[:, k, :]).then_inc(attention_high, 1)
                        dve.wait_ge(attention_high, 2 * i - 1 + b)
                        dve.tensor_tensor(ah[:, k, 1, :], attnf[:, k, :], ah[:, k, 0, :], ALU.subtract).then_inc(attention_low, 1)
                if front:
                    after(dve, ffn_scores_done, i + 1)
                    dve.tensor_reduce(smx[:, :], ps[:, 0:2, 0:8 * S].rearrange("p b (k j) -> p b k j", j=S), AX.X, ALU.max).then_inc(ffn_max_done, 1)
                    dve.wait_ge(ffn_max_done, i + 1)
                    after(dve, ffn_exps_done, i)
                    dve.tensor_tensor(ssub[:, :, :].rearrange("p (b k) j -> p b k j", b=2),
                                      ps[:, 0:2, 0:8 * S].rearrange("p b (k j) -> p b k j", j=S),
                                      smx[:, :].rearrange("p (b k) -> p b k", b=2).unsqueeze(3).broadcast_to((P, 2, K16, S)),
                                      ALU.subtract).then_inc(ffn_shifted, 1)
                if nxt:
                    top_two(i + 1)
                if back:
                    after(dve, output_done, i)
                    dve.tensor_tensor(y_all[:, bass.ds((i - 1) * C, C)], ps[:, 3, 0:C], x2_all[:, bass.ds((i - 1) * C, C)],
                                      ALU.add).then_inc(y_ready, 1)
                if nxt:
                    second(i + 1)

            dve.wait_ge(memsets_done, 23)
            dve.wait_ge(x2_kept, NP)
            normalise(0)
            top_two(0)
            second(0)
            iteration(0, back=False)
            iteration(1)
            with dve.Fori(2, NP - 1) as i:
                iteration(i)
            iteration(NP - 1, nxt=False)
            iteration(NP, front=False, nxt=False)

        @block.tensor
        def _(pe):
            pe.wait_ge(ident_ready, 2)
            pe.wait_ge(weights_loaded, 16 * NW)
            pe.transpose(ps[:, 0, 0:P], wq_nat[:, :], ident[:, :])
            pe.transpose(ps[:, 0, P:2 * P], wv_nat[:, :], ident[:, :]).then_inc(setup_product, 1)
            pe.wait_ge(bk_spread, 1)
            pe.matmul(ps[:, 1, 0:C], bk_rep[:, :], wq_nat[:, :], start=True, stop=True)
            pe.matmul(ps[:, 1, C:C + 1], bk_rep[:, :], bq_col[:, :], start=True, stop=True).then_inc(bk_products, 1)
            for g in range(NG):
                pe.wait_ge(ln1_done, g + 1)
                if g == NG - 1:
                    pe.wait_ge(setup_copied, 1)
                for k in range(4):
                    n = 4 * g + k
                    last = pe.transpose(ps[:, (5, 6, 7, 0)[g], P * k:P * k + P], y_all[:, C * n:C * n + C], ident[:, :])
                last.then_inc(setup_product, 1)
            pe.wait_ge(bk_products_out, 1)
            for g in range(NG):
                pe.wait_ge(setup_copied, 2 + g)
                pe.matmul(ps[:, 1 + g, 0:GW], wqT[:, :], xn1T[:, GW * g:GW * (g + 1)], start=True, stop=True).then_inc(setup_product, 1)
            for g in range(NG):
                pe.wait_ge(setup_copied, 2 + NG + g)
                pe.matmul(ps[:, (5, 6, 7, 0)[g], 0:GW], wk_nat[:, :], qT[:, 8 * g:8 * g + 8, 0:S], start=True, stop=True).then_inc(setup_product, 1)
            pe.wait_ge(consts_ready, 3)
            pe.wait_ge(qk_low_ready, NG)
            pe.wait_ge(memsets_done, 10)

            def turn(n, b, k, chunks=(0, 1, 2)):
                after(pe, ctx_high, n + 1)
                for c in chunks:
                    if c == 1:
                        after(pe, ctx_low, n + 1)
                    if c == 2:
                        after(pe, ctx_low_rest, n + 1)
                    if c == 0:
                        after(pe, tiles_copied_act, n)
                    elif c == 1:
                        after(pe, tiles_copied_dve, 2 * n)
                    else:
                        after(pe, tiles_copied_dve, 2 * n + 1)
                    for j in range(8 * c, 8 * c + 8):
                        last = pe.transpose(ps[:, (3 * b + c) % 2, :].bitcast(F16)[:, P * (j % 8):P * (j % 8) + P],
                                            nat[k][:, j // TK, C * (j % TK):C * (j % TK) + C], ident16[:, :])
                    last.then_inc(tiles_turned, 1)

            def scores(n, pair, s, b):
                after(pe, tiles_copied_dve, 2 * n + 2)
                after(pe, tiles_copied_act, n + 1)
                after(pe, qk_copied, pair + 1)
                after(pe, exps_done, 2 * n - 2)
                for t in range(TK):
                    o = ps[:, 2 + 2 * b + t // 6, S * (t % 6):S * (t % 6) + S]
                    hi = ctxT[b][:, P * t:P * t + P]
                    lo = ctxT[b][:, P * (TK + t):P * (TK + t) + P]
                    qh, ql = qk_cur[s][:, 0, S * b:S * b + S], qk_cur[s][:, 1, S * b:S * b + S]
                    pe.matmul(o, hi, qh, start=(t % 6 == 0), stop=False, skip_group_check=True)
                    pe.matmul(o, hi, ql, start=False, stop=False, skip_group_check=True)
                    last = pe.matmul(o, lo, qh, start=False, stop=False, skip_group_check=True)
                last.then_inc(scores_done, 1)

            def max_turn(pair):
                after(pe, tile_max_done, 2 * pair + 2)
                after(pe, query_max_done, pair)
                pe.transpose(ps[:, 7, 0:P], tmax[:, :, :].rearrange("p b q -> p (b q)"), ident[:, :]).then_inc(max_turned, 1)

            def shift(n, pair, b):
                after(pe, shift_low, pair + 1)
                for a in range(2):
                    o = ps[:, 2 + 2 * b + a, 0:6 * S].rearrange("p (t q) -> p t q", t=6)
                    for part in range(2):
                        last = pe.matmul(o, rows_of[:, b, :],
                                         dg[:, part, :].unsqueeze(1).broadcast_to((P, 6, S)),
                                         start=False, stop=(part == 1), skip_group_check=True)
                last.then_inc(scores_shifted, 1)

            def values(n, pair, b, k):
                after(pe, exps_low, n + 1)
                if b == 0:
                    after(pe, x2_done, pair)
                o = ps[:, 6, SLOT * b:SLOT * b + S]
                for t in range(TK):
                    r = slice(0, P if t < TK - 1 else REST)
                    hi, lo = nat[k][r, 0, C * t:C * t + C], nat[k][r, 1, C * t:C * t + C]
                    ph, pl = p16[r, 0, t, b, 0:S], p16[r, 1, t, b, 0:S]
                    pe.matmul(o, hi, ph, start=(t == 0), stop=False)
                    pe.matmul(o, hi, pl, start=False, stop=False)
                    last = pe.matmul(o, lo, ph, start=False, stop=(t == TK - 1))
                last.then_inc(values_done, 1)

            def denominator(pair):
                for part in range(2):
                    for t in range(TK):
                        r = slice(0, P if t < TK - 1 else REST)
                        last = pe.matmul(ps[:, 6, P:P + 1], p16[r, part, t, :, :].rearrange("p b q -> p (b q)"), ones16[r, :],
                                         start=(part == 0 and t == 0), stop=(part == 1 and t == TK - 1))
                last.then_inc(denominator_done, 1)

            def project(pair):
                after(pe, sums_copied, pair + 1)
                after(pe, denominator_inverted, pair + 1)
                pe.matmul(ps[:, 6, 2 * P:3 * P], aoT[:, :, :].rearrange("p b q -> p (b q)"), wvT[:, :], start=True, stop=True).then_inc(projection_done, 1)

            def steps(i):
                for s in range(2):
                    pair = 2 * i + s
                    n = 2 * pair
                    first = isinstance(pair, int) and pair == 0
                    more = not (isinstance(pair, int) and pair == NP - 1)
                    k0, k1 = (2 * s + 2) % 4, (2 * s + 3) % 4
                    scores(n, pair, s, 0)
                    scores(n + 1, pair, s, 1)
                    if not first:
                        values(n - 2, pair - 1, 0, k0)
                    max_turn(pair)
                    if not first:
                        values(n - 1, pair - 1, 1, k1)
                        denominator(pair - 1)
                    if more:
                        turn(n + 2, 0, k0, (0,))
                    shift(n, pair, 0)
                    if more:
                        turn(n + 2, 0, k0, (1,))
                    shift(n + 1, pair, 1)
                    if not first:
                        project(pair - 1)
                    if more:
                        turn(n + 2, 0, k0, (2,))
                        turn(n + 3, 1, k1, (0,))
                        turn(n + 3, 1, k1, (1,))
                        turn(n + 3, 1, k1, (2,))

            for b in range(2):
                turn(b, b, b)
            steps(0)
            with pe.Fori(1, NP // 2 - 1) as i:
                steps(i)
            steps(NP // 2 - 1)
            pe.wait_ge(ffn_weights_loaded, 16 * NFW)
            pe.wait_ge(tiles_copied_dve, 4 * NP)
            pe.wait_ge(tiles_copied_act, 2 * NP)
            for k in range(E // 2):
                last = pe.transpose(ps[:, 0, P * k:P * k + P], fwv_nat[:, k, :], ident[:, :])
            last.then_inc(ffn_w_product, 1)
            pe.transpose(ps[:, 1, 0:P], fws_nat[:, :], ident[:, :])
            pe.transpose(ps[:, 1, P:2 * P], fwd_nat[:, :], ident[:, :]).then_inc(ffn_w_product, 1)
            pe.wait_ge(exps_done, 4 * NP - 2)
            for e in range(E):
                last = pe.transpose(ps[:, 2 + e // 4, P * (e % 4):P * (e % 4) + P], fwo_nat[:, e, :, :].rearrange("p a d -> p (a d)"), ident[:, :])
            last.then_inc(ffn_w_product, 1)

            def head_products(h2):
                for a in range(2):
                    for k in range(4):
                        last = pe.matmul(ps[:, 4 * h2 + a, P * k:P * k + P], fwk_nat[DH * h2:DH * h2 + DH, 4 * a + k, :],
                                         fwq_nat[DH * h2:DH * h2 + DH, 4 * a + k, :], start=True, stop=True)
                last.then_inc(ffn_w_product, 1)

            values(2 * NP - 2, NP - 1, 0, 2)
            pe.wait_ge(ffn_w_copied, 2)
            head_products(0)
            values(2 * NP - 1, NP - 1, 1, 3)
            denominator(NP - 1)
            project(NP - 1)
            pe.wait_ge(exps_done, 4 * NP)
            head_products(1)

            def xn_turn(i):
                after(pe, xn_ready, i + 1)
                after(pe, z_second_copied, i)
                pe.transpose(ps[:, 2, 0:P], xn[:, :], ident[:, :]).then_inc(xn_turned, 1)

            def z_heads(h0, first_bank):
                for h in range(h0, h0 + 8):
                    k = h - h0
                    o = ps[:, first_bank + k // 4, 2 * S * (k % 4):2 * S * (k % 4) + 2 * S]
                    pe.matmul(o, mT[:, 0, h, :], xn16[:, 0, :], start=True, stop=False)
                    pe.matmul(o, mT[:, 0, h, :], xn16[:, 1, :], start=False, stop=False)
                    last = pe.matmul(o, mT[:, 1, h, :], xn16[:, 0, :], start=False, stop=True)
                return last

            def gates(i):
                after(pe, xnT_copied, i + 1)
                after(pe, xn_high, i + 1)
                for q in range(NQ):
                    for h4 in range(4):
                        last = pe.matmul(ps[32 * h4:32 * h4 + 32, 2, 64 * q:64 * q + 64], xnT[:, HALF * q:HALF * q + 32],
                                         wg[:, h4, :, :, :].rearrange("p g n e -> p (g n e)"), start=True, stop=True)
                last.then_inc(gates_done, 1)

            def iteration(i, front=True, back=True, nxt=True):
                if back:
                    after(pe, diagonals_dve, i)
                    after(pe, diagonals_pool, i)
                    after(pe, experts_low, i)
                    after(pe, experts_copied, i)
                    after(pe, attention_normalised, 2 * i - 2)
                    for q in range(NQ):
                        for k in (2 * q, 2 * q + 1):
                            for a, b in ((0, 0), (0, 1), (1, 0)):
                                for par in range(2):
                                    o = ps[DH * par:DH * par + DH, 6 + q // 2, 224 * (q % 2):224 * (q % 2) + 224].rearrange("p (t h) -> p t h", h=8)
                                    last = pe.matmul(o, pj[:, a, k, :], dv[:, b, k, :, 8 * par:8 * par + 8],
                                                     start=(k % 2 == 0 and a + b == 0), stop=(k % 2 == 1 and a == 1))
                    last.then_inc(mixed_done, 1)
                if front:
                    after(pe, y_ready, i - 1)
                    for q in range(NQ):
                        for e4 in range(4):
                            last = pe.matmul(ps[32 * e4:32 * e4 + 32, 3, P * q:P * q + P].rearrange("p (a d) -> p a d", a=2),
                                             xnT[:, HALF * q:HALF * q + 32],
                                             fwvT[:, e4::4, :], start=True, stop=True)
                    last.then_inc(experts_done, 1)
                    after(pe, exps_turned_copied, 2 * i)
                    after(pe, xn_low, i + 1)
                    z_heads(0, 0).then_inc(z_first_done, 1)
                    after(pe, mix_ready, i + 1)
                    after(pe, experts_copied, i + 1)
                    for h4 in range(4):
                        for e4 in range(4):
                            o = ps[32 * e4:32 * e4 + 32, 3, 0:P].rearrange("p (q a h) -> p q a h", q=NQ, a=2)
                            first = 8 * (h4 % 2) + h4 // 2
                            last = pe.matmul(o[:, :, :, first:first + 7:2], ident[:, 32 * h4:32 * h4 + 32],
                                             mix[:, :, :, e4::4].rearrange("p q n a -> p q a n"), start=True, stop=True)
                    last.then_inc(mix_moved, 1)
                if back:
                    after(pe, mixed_copied, i)
                    after(pe, masked_copied, i - 1)
                    for k in range(8):
                        last = pe.transpose(ps[:, 4 + k // 4, P * (k % 4):P * (k % 4) + P],
                                            vT[:, k, :, :].rearrange("p b t -> p (b t)"), ident[:, :])
                    last.then_inc(mixed_turned, 1)
                if front:
                    after(pe, gates_copied, i + 1)
                    after(pe, mix_copied, i + 1)
                    z_heads(8, 2).then_inc(z_second_done, 1)
                if back:
                    after(pe, exps_turned_copied, 2 * i)
                    after(pe, mixed_turned_copied, i)
                    for b in range(2):
                        for half in range(2):
                            for hg in range(HG):
                                for h4 in range(4):
                                    last = pe.matmul(ps[32 * h4:32 * h4 + 32, 6 + b, 256 * half + 64 * hg:256 * half + 64 * hg + 64],
                                                     eT[:, b, HG * half + hg, 32 * h4:32 * h4 + 32],
                                                     v_sb[:, 4 * hg + h4, :], start=True, stop=True)
                        last.then_inc(attention_done, 1)
                if front:
                    after(pe, z_first_copied, i + 1)
                    after(pe, z_second_copied, i + 1)
                    for q in range(NQ):
                        b = q // 2
                        for h4 in range(4):
                            last = pe.matmul(ps[32 * h4:32 * h4 + 32, b, 224 * (q % 2):224 * (q % 2) + 224].rearrange("p (n j) -> p n j", j=S),
                                             xnT[:, HALF * q:HALF * q + 32], z[:, h4::4, S * b:S * b + S], start=True, stop=True)
                    last.then_inc(ffn_scores_done, 1)
                if nxt:
                    xn_turn(i + 1)
                if back:
                    after(pe, masks_ready, i)
                    for q in range(NQ):
                        if q % 2 == 0:
                            after(pe, attention_low, 2 * i - 1 + q // 2)
                        for hg in range(HG):
                            n = HG * q + hg
                            last = pe.matmul(ps[:, 4 + q // 2, 224 * (q % 2):224 * (q % 2) + 224], ah[:, n, :, :].rearrange("p a d -> p (a d)"),
                                             dm[:, n, :, :].rearrange("p t e -> p (t e)"), start=(hg == 0), stop=(hg == HG - 1))
                    last.then_inc(masked_done, 1)
                if nxt:
                    gates(i + 1)
                if back:
                    after(pe, masked_copied, i)
                    if front:
                        after(pe, z_second_copied, i + 1)
                    for e in range(E):
                        last = pe.matmul(ps[:, 3, 0:C], aT[:, e, :, :].rearrange("p b t -> p (b t)"), wo2[:, e, :],
                                         start=(e == 0), stop=(e == E - 1))
                    last.then_inc(output_done, 1)
                if front:
                    after(pe, ffn_exps_done, i + 1)
                    after(pe, ffn_shifted, i + 1)
                    for k in range(K16):
                        last = pe.transpose(ps[:, k // 4, P * (k % 4):P * (k % 4) + P],
                                            e_sb[:, k, :, :].rearrange("p b j -> p (b j)"), ident[:, :])
                    last.then_inc(exps_turned, 1)

            pe.wait_ge(x2_moments_kept, NP)
            pe.wait_ge(ffn_w_copied, 5)
            pe.wait_ge(ffn_w_low, 2)
            xn_turn(0)
            gates(0)
            iteration(0, back=False)
            iteration(1)
            with pe.Fori(2, NP - 1) as i:
                iteration(i)
            iteration(NP - 1, nxt=False)
            iteration(NP, front=False, nxt=False)


_INS = ['x', 'ctx_1024', 'L0_xattn_Wq', 'L0_xattn_bq', 'L0_xattn_Wk', 'L0_xattn_bk', 'L0_xattn_Wv', 'L0_xattn_bv',
        'L0_ffn_Wq', 'L0_ffn_Wk', 'L0_ffn_Wv', 'L0_ffn_Ws', 'L0_ffn_Wd', 'L0_ffn_Wo']
_OUTS = [((32, 56, 128), 'float32')]


def kernel(**inputs):
    import numpy as _np
    import concourse.bacc as _bacc
    from concourse import mybir as _mybir
    from concourse.bass_utils import run_bass_kernel_spmd as _run

    nc = _bacc.Bacc("TRN2", target_bir_lowering=False, num_devices=1)
    arrays, args = {}, []
    for name in _INS:
        a = _np.ascontiguousarray(inputs[name])
        arrays[f"in_{name}_dram"] = a
        args.append(nc.dram_tensor(f"in_{name}_dram", a.shape, _mybir.dt.from_np(a.dtype), kind="ExternalInput").ap())
    for i, (shape, dtype) in enumerate(_OUTS):
        dt = _mybir.dt.from_np(_np.dtype(dtype))
        args.append(nc.dram_tensor(f"out_{i}_dram", shape, dt, kind="ExternalOutput").ap())
    xattn_ffn(nc, *args)
    r = _run(nc, [arrays], core_ids=[0])
    return r.results[0]["out_0_dram"]
```
